# Optimizing a Trainium2 kernel written in Bass

```python
import numpy as np
import jax
import jax.numpy as jnp

def _softmax(x, axis=-1):
    return jax.nn.softmax(x, axis=axis)

def _gelu(x):
    return jax.nn.gelu(x, approximate=True)

def _silu(x):
    return jax.nn.silu(x)

def _sigmoid(x):
    return jax.nn.sigmoid(x)

def _layernorm(x, axis=-1, eps=1e-05):
    m = jnp.mean(x, axis=axis, keepdims=True)
    v = jnp.var(x, axis=axis, keepdims=True)
    return (x - m) / jnp.sqrt(v + eps)

def _scatter_add(tgt, idx, src, axis=0):
    return tgt.at[idx].add(src)

def _segment_sum(src, seg, n):
    return jax.ops.segment_sum(src, seg, n)
kernel_name = 'mk_adaln_d2_jaxref_r8_817512'

def setup_inputs(seed: int=0):
    np.random.seed(seed)
    _w = jnp.asarray

    def _L0_attn_setup():
        import jax, jax.numpy as jnp
        import numpy as np
        import math
        D_MODEL, D_C, D_R, NH = (128, 128, 32, 16)
        HD = D_MODEL // NH
        B, T = (2, 256)

        def _rope_tables(T, d_R):
            inv_freq = 1.0 / 10000.0 ** (jnp.arange(0, d_R, 2, dtype=jnp.float32) / d_R)
            t = jnp.arange(T, dtype=jnp.float32)
            freqs = jnp.outer(t, inv_freq)
            return (jnp.cos(freqs), jnp.sin(freqs))

        def _rotary_apply(x, cos, sin):
            d = x.shape[-1]
            x1, x2 = (x[..., :d // 2], x[..., d // 2:])
            return jnp.concatenate([x1 * cos - x2 * sin, x2 * cos + x1 * sin], axis=-1)
        key = jax.random.key(seed)
        ks = jax.random.split(key, 8)
        s = lambda fan_in: 1.0 / math.sqrt(fan_in)
        return {'x': jax.random.normal(ks[0], (B, T, D_MODEL), jnp.float32), 'W_kv_down': jax.random.normal(ks[1], (D_MODEL, D_C), jnp.float32) * s(D_MODEL), 'W_k_up': jax.random.normal(ks[2], (D_C, D_MODEL), jnp.float32) * s(D_C), 'W_v_up': jax.random.normal(ks[3], (D_C, D_MODEL), jnp.float32) * s(D_C), 'W_q': jax.random.normal(ks[4], (D_MODEL, D_MODEL), jnp.float32) * s(D_MODEL), 'W_q_rope': jax.random.normal(ks[5], (D_MODEL, D_R), jnp.float32) * s(D_MODEL), 'W_k_rope': jax.random.normal(ks[6], (D_C, D_R), jnp.float32) * s(D_C), 'W_o': jax.random.normal(ks[7], (D_MODEL, D_MODEL), jnp.float32) * s(D_MODEL)}
    _L0_attn_in = _L0_attn_setup()

    def _L0_ffn_setup():
        import jax, jax.numpy as jnp
        import numpy as np
        D_MODEL = 128
        D_FF = 512
        NUM_M = 2
        E_ROUTER = 8 * NUM_M - 1
        D_FF_R = D_FF // NUM_M
        TOP_K = NUM_M * 2 - 1
        B, T = (2, 256)

        def _expert_stack(x, W1, b1, W2, b2):
            h = jax.nn.gelu(jnp.einsum('btd,edf->ebtf', x, W1) + b1[:, None, None, :], approximate=False)
            return jnp.einsum('ebtf,efd->ebtd', h, W2) + b2[:, None, None, :]
        key = jax.random.key(seed)
        ks = jax.random.split(key, 12)
        s = lambda fan_in: 1.0 / np.sqrt(fan_in)
        x = jax.random.normal(ks[0], (B, T, D_MODEL), dtype=jnp.float32)
        sW1 = jax.random.uniform(ks[1], (1, D_MODEL, D_FF), jnp.float32, -s(D_MODEL), s(D_MODEL))
        sb1 = jax.random.uniform(ks[2], (1, D_FF), jnp.float32, -s(D_MODEL), s(D_MODEL))
        sW2 = jax.random.uniform(ks[3], (1, D_FF, D_MODEL), jnp.float32, -s(D_FF), s(D_FF))
        sb2 = jax.random.uniform(ks[4], (1, D_MODEL), jnp.float32, -s(D_FF), s(D_FF))
        rW1 = jax.random.uniform(ks[5], (E_ROUTER, D_MODEL, D_FF_R), jnp.float32, -s(D_MODEL), s(D_MODEL))
        rb1 = jax.random.uniform(ks[6], (E_ROUTER, D_FF_R), jnp.float32, -s(D_MODEL), s(D_MODEL))
        rW2 = jax.random.uniform(ks[7], (E_ROUTER, D_FF_R, D_MODEL), jnp.float32, -s(D_FF_R), s(D_FF_R))
        rb2 = jax.random.uniform(ks[8], (E_ROUTER, D_MODEL), jnp.float32, -s(D_FF_R), s(D_FF_R))
        gW = jax.random.uniform(ks[9], (D_MODEL, E_ROUTER), jnp.float32, -s(D_MODEL), s(D_MODEL))
        gb = jax.random.uniform(ks[10], (E_ROUTER,), jnp.float32, -s(D_MODEL), s(D_MODEL))
        return {'x': x, 'sW1': sW1, 'sb1': sb1, 'sW2': sW2, 'sb2': sb2, 'rW1': rW1, 'rb1': rb1, 'rW2': rW2, 'rb2': rb2, 'gW': gW, 'gb': gb}
    _L0_ffn_in = _L0_ffn_setup()
    _L0_c = _w((lambda *s: np.random.randn(*s).astype(np.float32) * 0.05)(4, 128))
    _L0_wmod = _w((lambda *s: np.random.randn(*s).astype(np.float32) * 0.05)(128, 6 * 128) * 128 ** (-0.5))

    def _L1_attn_setup():
        import jax, jax.numpy as jnp
        import numpy as np
        DIM = 128
        NUM_HEADS = 16
        NUM_GROUPS = 8

        def grouped_linear(x, w, b):
            B, N, Cin = x.shape
            G = w.shape[0]
            xg = x.reshape(B, N, G, Cin // G)
            out = jnp.einsum('bngi,gio->bngo', xg, w)
            out = out.reshape(B, N, -1)
            if b is not None:
                out = out + b
            return out
        key = jax.random.key(seed)
        k1, k2, k3, k4 = jax.random.split(key, 4)
        G = NUM_GROUPS
        x = jax.random.normal(k1, (2, 256, DIM), dtype=jnp.float32)
        w_qkv = jax.random.normal(k2, (G, DIM // G, 3 * DIM // G), dtype=jnp.float32) * (DIM // G) ** (-0.5)
        w_proj = jax.random.normal(k3, (G, DIM // G, DIM // G), dtype=jnp.float32) * (DIM // G) ** (-0.5)
        b_proj = jax.random.normal(k4, (DIM,), dtype=jnp.float32) * 0.02
        return {'x': x, 'w_qkv': w_qkv, 'w_proj': w_proj, 'b_proj': b_proj}
    _L1_attn_in = _L1_attn_setup()

    def _L1_ffn_setup():
        import jax, jax.numpy as jnp
        import numpy as np
        B, S, D, F, E = (4, 256, 128, 512, 8)
        LN_EPS = 1e-05
        key = jax.random.key(seed)
        ks = jax.random.split(key, 6)
        sc = 0.02
        return {'x': jax.random.normal(ks[0], (B, S, D), dtype=jnp.float32), 'Wr': jax.random.normal(ks[1], (D, E), dtype=jnp.float32) * sc, 'br': jnp.zeros((E,), jnp.float32), 'ln_g': jnp.ones((D,), jnp.float32), 'ln_b': jnp.zeros((D,), jnp.float32), 'W1': jax.random.normal(ks[2], (E, D, F), dtype=jnp.float32) * sc, 'b1': jnp.zeros((E, F), jnp.float32), 'W2': jax.random.normal(ks[3], (E, F, D), dtype=jnp.float32) * sc, 'b2': jnp.zeros((E, D), jnp.float32)}
    _L1_ffn_in = _L1_ffn_setup()
    _L1_c = _w((lambda *s: np.random.randn(*s).astype(np.float32) * 0.05)(4, 128))
    _L1_wmod = _w((lambda *s: np.random.randn(*s).astype(np.float32) * 0.05)(128, 6 * 128) * 128 ** (-0.5))
    _d = {'L0_attn_x': _L0_attn_in['x'], 'L0_attn_W_kv_down': _L0_attn_in['W_kv_down'], 'L0_attn_W_k_up': _L0_attn_in['W_k_up'], 'L0_attn_W_v_up': _L0_attn_in['W_v_up'], 'L0_attn_W_q': _L0_attn_in['W_q'], 'L0_attn_W_q_rope': _L0_attn_in['W_q_rope'], 'L0_attn_W_k_rope': _L0_attn_in['W_k_rope'], 'L0_attn_W_o': _L0_attn_in['W_o'], 'L0_ffn_sW1': _L0_ffn_in['sW1'], 'L0_ffn_sb1': _L0_ffn_in['sb1'], 'L0_ffn_sW2': _L0_ffn_in['sW2'], 'L0_ffn_sb2': _L0_ffn_in['sb2'], 'L0_ffn_rW1': _L0_ffn_in['rW1'], 'L0_ffn_rb1': _L0_ffn_in['rb1'], 'L0_ffn_rW2': _L0_ffn_in['rW2'], 'L0_ffn_rb2': _L0_ffn_in['rb2'], 'L0_ffn_gW': _L0_ffn_in['gW'], 'L0_ffn_gb': _L0_ffn_in['gb'], 'L0_c': _L0_c, 'L0_wmod': _L0_wmod, 'L1_attn_w_qkv': _L1_attn_in['w_qkv'], 'L1_attn_w_proj': _L1_attn_in['w_proj'], 'L1_attn_b_proj': _L1_attn_in['b_proj'], 'L1_ffn_Wr': _L1_ffn_in['Wr'], 'L1_ffn_br': _L1_ffn_in['br'], 'L1_ffn_ln_g': _L1_ffn_in['ln_g'], 'L1_ffn_ln_b': _L1_ffn_in['ln_b'], 'L1_ffn_W1': _L1_ffn_in['W1'], 'L1_ffn_b1': _L1_ffn_in['b1'], 'L1_ffn_W2': _L1_ffn_in['W2'], 'L1_ffn_b2': _L1_ffn_in['b2'], 'L1_c': _L1_c, 'L1_wmod': _L1_wmod}
    _x0 = _d['L0_attn_x']
    _d['L0_attn_x'] = jax.random.normal(jax.random.fold_in(jax.random.key(seed), 1), (4, 512, 128), dtype=_x0.dtype)
    del _x0
    return _d

def reference(L0_attn_x, L0_attn_W_kv_down, L0_attn_W_k_up, L0_attn_W_v_up, L0_attn_W_q, L0_attn_W_q_rope, L0_attn_W_k_rope, L0_attn_W_o, L0_ffn_sW1, L0_ffn_sb1, L0_ffn_sW2, L0_ffn_sb2, L0_ffn_rW1, L0_ffn_rb1, L0_ffn_rW2, L0_ffn_rb2, L0_ffn_gW, L0_ffn_gb, L0_c, L0_wmod, L1_attn_w_qkv, L1_attn_w_proj, L1_attn_b_proj, L1_ffn_Wr, L1_ffn_br, L1_ffn_ln_g, L1_ffn_ln_b, L1_ffn_W1, L1_ffn_b1, L1_ffn_W2, L1_ffn_b2, L1_c, L1_wmod):

    def _L0_attn_ref(x, W_kv_down, W_k_up, W_v_up, W_q, W_q_rope, W_k_rope, W_o):
        import jax, jax.numpy as jnp
        import numpy as np
        import math
        D_MODEL, D_C, D_R, NH = (128, 128, 32, 16)
        HD = D_MODEL // NH
        B, T = (2, 256)

        def _rope_tables(T, d_R):
            inv_freq = 1.0 / 10000.0 ** (jnp.arange(0, d_R, 2, dtype=jnp.float32) / d_R)
            t = jnp.arange(T, dtype=jnp.float32)
            freqs = jnp.outer(t, inv_freq)
            return (jnp.cos(freqs), jnp.sin(freqs))

        def _rotary_apply(x, cos, sin):
            d = x.shape[-1]
            x1, x2 = (x[..., :d // 2], x[..., d // 2:])
            return jnp.concatenate([x1 * cos - x2 * sin, x2 * cos + x1 * sin], axis=-1)
        Bb, Tt, _ = x.shape
        cos, sin = _rope_tables(Tt, D_R)
        cos = cos[None]
        sin = sin[None]
        c_kv = x @ W_kv_down
        k_rope = _rotary_apply(c_kv @ W_k_rope, cos, sin)
        k = (c_kv @ W_k_up).reshape(Bb, Tt, NH, HD)
        v = (c_kv @ W_v_up).reshape(Bb, Tt, NH, HD)
        q = (x @ W_q).reshape(Bb, Tt, NH, HD)
        q_rope = _rotary_apply(x @ W_q_rope, cos, sin)
        scale = math.sqrt(HD + D_R)
        scores = jnp.einsum('bqhd,bkhd->bhqk', q, k)
        scores = scores + jnp.einsum('bqr,bkr->bqk', q_rope, k_rope)[:, None]
        scores = scores / scale
        causal = jnp.triu(jnp.ones((Tt, Tt), dtype=bool), k=1)
        scores = jnp.where(causal[None, None], -jnp.inf, scores)
        w = jax.nn.softmax(scores, axis=-1)
        attn = jnp.einsum('bhqk,bkhd->bqhd', w, v).reshape(Bb, Tt, D_MODEL)
        return attn @ W_o

    def _L0_ffn_ref(x, sW1, sb1, sW2, sb2, rW1, rb1, rW2, rb2, gW, gb):
        import jax, jax.numpy as jnp
        import numpy as np
        D_MODEL = 128
        D_FF = 512
        NUM_M = 2
        E_ROUTER = 8 * NUM_M - 1
        D_FF_R = D_FF // NUM_M
        TOP_K = NUM_M * 2 - 1
        B, T = (2, 256)

        def _expert_stack(x, W1, b1, W2, b2):
            h = jax.nn.gelu(jnp.einsum('btd,edf->ebtf', x, W1) + b1[:, None, None, :], approximate=False)
            return jnp.einsum('ebtf,efd->ebtd', h, W2) + b2[:, None, None, :]
        shared_enc = _expert_stack(x, sW1, sb1, sW2, sb2).sum(0)
        weights = jax.nn.softmax(x @ gW + gb, axis=-1)
        topv, topi = jax.lax.top_k(weights, TOP_K)
        gated = (jax.nn.one_hot(topi, E_ROUTER, dtype=weights.dtype) * topv[..., None]).sum(axis=-2)
        router_out = _expert_stack(x, rW1, rb1, rW2, rb2)
        router_enc = jnp.einsum('ebtd,bte->btd', router_out, gated)
        return shared_enc + router_enc + x

    def _L1_attn_ref(x, w_qkv, w_proj, b_proj):
        import jax, jax.numpy as jnp
        import numpy as np
        DIM = 128
        NUM_HEADS = 16
        NUM_GROUPS = 8

        def grouped_linear(x, w, b):
            B, N, Cin = x.shape
            G = w.shape[0]
            xg = x.reshape(B, N, G, Cin // G)
            out = jnp.einsum('bngi,gio->bngo', xg, w)
            out = out.reshape(B, N, -1)
            if b is not None:
                out = out + b
            return out
        B, N, C = x.shape
        H = NUM_HEADS
        D = C // H
        scale = D ** (-0.5)
        qkv = grouped_linear(x, w_qkv, None)
        qkv = qkv.reshape(B, N, 3, H, D)
        qkv = jnp.transpose(qkv, (2, 0, 3, 1, 4))
        q, k, v = (qkv[0] * scale, qkv[1], qkv[2])
        attn = jnp.einsum('bhnd,bhmd->bhnm', q, k)
        attn = jax.nn.softmax(attn, axis=-1)
        out = jnp.einsum('bhnm,bhmd->bhnd', attn, v)
        out = jnp.transpose(out, (0, 2, 1, 3)).reshape(B, N, C)
        out = grouped_linear(out, w_proj, b_proj)
        return out

    def _L1_ffn_ref(x, Wr, br, ln_g, ln_b, W1, b1, W2, b2):
        import jax, jax.numpy as jnp
        import numpy as np
        B, S, D, F, E = (4, 256, 128, 512, 8)
        LN_EPS = 1e-05
        tokens_shape = x.shape[:-1]
        xt = x.reshape(-1, x.shape[-1])
        router_logits = xt @ Wr + br
        router_probs = jax.nn.softmax(router_logits, axis=-1)
        gates = jnp.max(router_probs, axis=-1, keepdims=True)
        idx = jnp.argmax(router_probs, axis=-1)
        onehot = jax.nn.one_hot(idx, E, dtype=xt.dtype)
        mu = jnp.mean(xt, axis=-1, keepdims=True)
        var = jnp.mean(jnp.square(xt - mu), axis=-1, keepdims=True)
        xn = (xt - mu) * jax.lax.rsqrt(var + LN_EPS) * ln_g + ln_b
        h = jnp.einsum('te,td,edf->tf', onehot, xn, W1) + b1[idx]
        h = jax.nn.relu(h)
        y = jnp.einsum('te,tf,efd->td', onehot, h, W2) + b2[idx]
        y = y * gates
        return y.reshape(tokens_shape + (y.shape[-1],))
    x = L0_attn_x
    mod = (_silu(L0_c) @ L0_wmod).reshape(L0_c.shape[0], 6, 1, -1)
    sa, ca, ga, sb, cb, gb = (mod[:, 0], mod[:, 1], mod[:, 2], mod[:, 3], mod[:, 4], mod[:, 5])
    ga = (2 * (ga >= 0) - 1) * jnp.maximum(jnp.abs(ga), 0.25)
    gb = (2 * (gb >= 0) - 1) * jnp.maximum(jnp.abs(gb), 0.25)
    h = _layernorm(x, axis=-1) * (1 + ca) + sa
    x = x + ga * _L0_attn_ref(h, L0_attn_W_kv_down, L0_attn_W_k_up, L0_attn_W_v_up, L0_attn_W_q, L0_attn_W_q_rope, L0_attn_W_k_rope, L0_attn_W_o)
    h = _layernorm(x, axis=-1) * (1 + cb) + sb
    x = x + gb * _L0_ffn_ref(h, L0_ffn_sW1, L0_ffn_sb1, L0_ffn_sW2, L0_ffn_sb2, L0_ffn_rW1, L0_ffn_rb1, L0_ffn_rW2, L0_ffn_rb2, L0_ffn_gW, L0_ffn_gb)
    mod = (_silu(L1_c) @ L1_wmod).reshape(L1_c.shape[0], 6, 1, -1)
    sa, ca, ga, sb, cb, gb = (mod[:, 0], mod[:, 1], mod[:, 2], mod[:, 3], mod[:, 4], mod[:, 5])
    ga = (2 * (ga >= 0) - 1) * jnp.maximum(jnp.abs(ga), 0.25)
    gb = (2 * (gb >= 0) - 1) * jnp.maximum(jnp.abs(gb), 0.25)
    h = _layernorm(x, axis=-1) * (1 + ca) + sa
    x = x + ga * _L1_attn_ref(h, L1_attn_w_qkv, L1_attn_w_proj, L1_attn_b_proj)
    h = _layernorm(x, axis=-1) * (1 + cb) + sb
    x = x + gb * _L1_ffn_ref(h, L1_ffn_Wr, L1_ffn_br, L1_ffn_ln_g, L1_ffn_ln_b, L1_ffn_W1, L1_ffn_b1, L1_ffn_W2, L1_ffn_b2)
    return x

_drawn_inputs = setup_inputs


def setup_inputs(seed=0):
    import zlib

    import numpy as np

    out = dict(_drawn_inputs(seed))
    spreads = {'L1_ffn_br': (0.0, 0.8),
     'L1_ffn_ln_g': (1.0, 0.6),
     'L1_ffn_ln_b': (0.0, 0.8),
     'L1_ffn_b1': (0.0, 0.8),
     'L1_ffn_b2': (0.0, 0.8)}
    factors = {'L0_attn_W_k_up': 2.786,
     'L0_attn_W_q': 2.798,
     'L0_ffn_sb1': 8.0,
     'L0_ffn_sb2': 8.0,
     'L0_ffn_rW1': 5.386,
     'L0_ffn_rb1': 8.0,
     'L0_ffn_rW2': 5.078,
     'L0_ffn_rb2': 8.0,
     'L0_ffn_gW': 5.532,
     'L0_ffn_gb': 8.0,
     'L1_attn_b_proj': 8.0,
     'L1_ffn_Wr': 8.0,
     'L1_ffn_W1': 8.0,
     'L1_ffn_W2': 8.0}
    for name, (base, spread) in spreads.items():
        noise = np.random.default_rng([zlib.crc32(name.encode()), seed]).standard_normal(out[name].shape)
        drawn = base * np.exp(spread * noise) if base else spread * noise
        out[name] = jnp.asarray(drawn.astype(out[name].dtype))
    for name, factor in factors.items():
        out[name] = (out[name] * factor).astype(out[name].dtype)
    return out
```

```python
from contextlib import ExitStack

import concourse.bass as bass
import numpy as np
from concourse import mybir

F32 = mybir.dt.float32
F32R = mybir.dt.float32r
BF16 = mybir.dt.bfloat16
I32 = mybir.dt.int32
ALU = mybir.AluOpType
ACT = mybir.ActivationFunctionType
AX = mybir.AxisListType

P = 128
NB, T, D = 4, 512, 128
NT = T // P
H, HD = 16, 8
DR = 32
NG, GH = 4, 4
E0, E1 = 15, 8
TOP = 3
C0, C1 = 2 * E0 + 4, 4 * E1
TERMS = 3
STACK = TERMS * GH * HD
ROPE = TERMS * DR
NOPE = TERMS * HD
K0 = ROPE + NOPE + 2
K1 = STACK + 2 * GH
SETS = 3
SCALE0 = 1.0 / float(np.sqrt(HD + DR))
SCALE1 = float(HD) ** -0.5
MASKED = -1e30
EPS = 1e-5

C_ID, C_MS, C_MT, C_HM, C_SG = 0, P, 2 * P, 3 * P, 3 * P + GH
C_COS = C_SG + 12
C_SIN = C_COS + T
C_N = C_SIN + T
SG_Q1, SG_K1, SG_QN, SG_KN, SG_QR, SG_KR = range(6)
R_B0, R_B1, R_LNG, R_LNB, R_C = 0, C0, C0 + C1, C0 + C1 + 1, C0 + C1 + 2
R_N = R_C + 2 * NB
V_STEPS = 109


def constants():
    c = np.zeros((P, C_N), np.float32)
    p = np.arange(P)
    c[:, C_ID:C_ID + P] = np.eye(P)
    c[:, C_MS:C_MS + P] = np.where(p[None, :] > p[:, None], MASKED, 0)
    c[:, C_MT:C_MT + P] = np.where(p[:, None] > p[None, :], MASKED, 0)
    for j in range(GH):
        own = ((p < STACK) & (p % (GH * HD) // HD == j)) | (p == STACK + j) | (p == STACK + GH + j)
        c[:, C_HM + j] = own

    def split(n, low, scale):
        c[:, C_SG + 2 * n] = np.where(low, -scale, scale)
        c[:, C_SG + 2 * n + 1] = np.where(low, scale, 0)

    split(SG_Q1, p // (GH * HD) == 2, SCALE1)
    split(SG_K1, p // (GH * HD) == 1, 1.0)
    split(SG_QN, p % NOPE // HD == 2, SCALE0)
    split(SG_KN, p % NOPE // HD == 1, 1.0)
    split(SG_QR, p // DR == 2, SCALE0)
    split(SG_KR, p // DR == 1, 1.0)
    inv = (np.float32(1.0) / np.float32(10000.0) ** (np.arange(0, DR, 2, dtype=np.float32) / np.float32(DR))).astype(np.float32)
    f = np.outer(np.arange(T, dtype=np.float32), inv).astype(np.float32).T
    c[:ROPE, C_COS:C_COS + T] = np.tile(np.cos(f), (2 * TERMS, 1))
    c[:ROPE, C_SIN:C_SIN + T] = np.tile(np.concatenate([-np.sin(f), np.sin(f)]), (TERMS, 1))
    return c


class Signal:

    def __init__(self, sem, per):
        self.sem, self.per, self.made = sem, per, 0

    def _wait(self, eng, value):
        eng.wait_ge(self.sem, value + 1)
        if eng.engine == mybir.EngineType.SP:
            eng.nop(nofuse=True)

    def by(self, ins):
        ins.then_inc(self.sem, 1)
        self.made += 1
        return ins

    def wait(self, eng, b, k=None):
        self._wait(eng, b * self.per + (self.per if k is None else k))

    def wait_before(self, eng, b):
        self._wait(eng, b * self.per)


class Ring:

    def __init__(self, sig, name, order, slots):
        self.where, n = {}, [0] * slots
        for i, unit in enumerate(order):
            assert unit not in self.where, unit
            self.where[unit] = (i % slots, n[i % slots])
            n[i % slots] += 1
        self.full = [sig(f"{name}{s}_full", n[s]) for s in range(slots)]
        self.taken = [sig(f"{name}{s}_taken", n[s]) for s in range(slots)]

    def open(self, eng, b, unit):
        s, k = self.where[unit]
        self.taken[s].wait(eng, b, k)
        return s

    def fill(self, unit, ins):
        self.full[self.where[unit][0]].by(ins)

    def wait(self, eng, b, unit):
        s, k = self.where[unit]
        self.full[s].wait(eng, b, k + 1)
        return s

    def take(self, unit, ins):
        self.taken[self.where[unit][0]].by(ins)

    def wait_taken(self, eng, b, unit):
        s, k = self.where[unit]
        self.taken[s].wait(eng, b, k + 1)

    def wait_full_before(self, eng, b):
        for f in self.full:
            f.wait_before(eng, b)


NS = NG * (GH // 2) * NT
NQ = NG * NT
AHEAD = [16, 10]
S_PACE = [[2, 2, 2, 2, 0, 0, 3, 3, 2, 0, 0, 0, 0, 0, 0, 0],
          [3, 3, 0, 0, 3, 3, 2, 0, 3, 3, 2, 0, 0, 0, 0, 0]]
MT_AT = [{1: 1, 5: 2, 10: 3}, {3: 1, 7: 2, 11: 3}]
OT_AT = {6: 0, 9: 1, 13: 2}
CU = [C0 // 2, C1 // 2]
EX = [E0, E1]


def pair_order():
    out = []
    for L in range(2):
        out.append(("ln1", L))
        if L == 0:
            out += ["ckv", ("rope", 0), ("rope", 1)]
        out += [("heads", L, g) for g in range(NG)] + [("v", L)]
        out += [("S", L, n) for n in range(NS)]
        out.append(("ln2", L))
        if L == 1:
            out.append("ln3")
        out += [("h", L, i) for i in range(CU[L])]
    return out


def single_order():
    out = []
    for L in range(2):
        out += [("ST", L, n) for n in range(NQ * GH)]
        out += [("Y", L, e) for e in range(EX[L] + 1)]
    return out


def s_of(L, q):
    first = AHEAD[L] + sum(S_PACE[L][:q])
    return list(range(first, first + S_PACE[L][q]))


def misc_order():
    out = []
    for L in range(2):
        out += [("bc", L), ("mt", L, 0)]
        for q in range(NQ):
            if q in MT_AT[L]:
                out.append(("mt", L, MT_AT[L][q]))
            if q in OT_AT:
                out.append(("ot", L, OT_AT[q]))
        out += [("ot", L, NG - 1), ("on", L), ("proj", L), ("lg", L), ("gt", L)]
    return out


def chunks_of(L, e):
    if L == 0:
        return list(range(2 * e, 2 * e + 2)) if e < E0 else list(range(2 * E0, C0))
    return list(range(4 * e, 4 * e + 4)) if e < E1 else []


def build(nc, a, out):
    ctx = ExitStack()
    with ctx:
        def sb(name, shape, dt=F32):
            return ctx.enter_context(nc.sbuf_tensor(name, shape, dt))

        def sem(name):
            return ctx.enter_context(nc.semaphore(name))

        signals = {}

        def sig(name, per):
            signals[name] = Signal(sem(name), per)
            return signals[name]

        cst = sb("cst", [P, C_N])
        rows = sb("rows", [R_N, P])
        cols = sb("cols", [P, R_N])
        w_kvd, w_kup, w_vup, w_q, w_o = (sb(n, [P, P]) for n in ("w_kvd", "w_kup", "w_vup", "w_q", "w_o"))
        w_rr = sb("w_rr", [P, 2, DR])
        w_rope = sb("w_rope", [P, 2, 2, ROPE])
        w_head0 = sb("w_head0", [P, 2, H, NOPE])
        w_qkv = sb("w_qkv", [P, 3 * D])
        w_proj = sb("w_proj", [P, D])
        w_head1 = sb("w_head1", [P, 2, NG, STACK])
        w1 = [sb("w1_0", [P, C0, P]), sb("w1_1", [P, C1, P])]
        w2 = [sb("w2_0", [P, C0, D]), sb("w2_1", [P, C1, D])]
        w_mod = sb("w_mod", [P, 2, 6, D])
        w_rt = [sb("w_rt0", [P, E0]), sb("w_rt1", [P, E1])]
        b_rt = [sb("b_rt0", [P, E0]), sb("b_rt1", [P, E1])]
        b_2 = [sb("b_20", [E0 + 1, D]), sb("b_21", [E1, D])]
        b_proj = sb("b_proj", [P, D])
        id_bf = sb("id_bf", [P, P], BF16)
        mask_bf = sb("mask_bf", [P, 2, P], BF16)
        silu = sb("silu", [P, 3, 2 * NB])
        modT = sb("modT", [P, 2, 6, NB])
        x = sb("x", [P, NB, NT, D])
        silu_b = sb("silu_b", [P, P])
        bc = [sb("bc0", [P, 4, D]), sb("bc1", [P, 4, D])]
        gsign = sb("gsign", [P, 2, D])
        stats = sb("stats", [P, NT, 6])
        mv = sb("mv", [P, NT, 2])
        nwt = sb("nwt", [P, 3, NT])
        xn = sb("xn", [P, NT, D])
        hT = sb("hT", [P, T])
        hT2 = sb("hT2", [P, T])
        ckvT = sb("ckvT", [P, T])
        q_op = sb("q_op", [P, SETS * GH, T])
        k_op = sb("k_op", [P, SETS * GH, T])
        stk = sb("stk", [P, 4, T])
        vaug = sb("vaug", [P, NT, H, 32])
        ring = sb("ring", [P, 8, T])
        mneg = sb("mneg", [P, 2, NT, GH])
        mrow0 = sb("mrow0", [P, 2, GH, NT])
        mrow1 = sb("mrow1", [P, NT, K1])
        mT = sb("mT", [2 * GH * NT, P])
        oT = sb("oT", [P, T])
        rsum = sb("rsum", [P, NT, GH])
        onorm = sb("onorm", [P, NT, D])
        acc = sb("acc", [P, NT, D])
        lg = sb("lg", [P, NT, 16])
        pw = sb("pw", [P, NT, 24])
        pr = sb("pr", [P, NT, 24])
        rmax = sb("rmax", [P, 2, NT])
        top = sb("top", [P, NT, 8])
        topk = [sb("topk0", [P, NT, 8]), sb("topk1", [P, NT, 8])]
        gate = sb("gate", [P, NT, 16])
        gateT = sb("gateT", [16, T])
        rot_a, rot_b, rot = (ring[0:ROPE, i, :] for i in range(3))
        rope_op = [ring[0:ROPE, 3, :], ring[0:ROPE, 4, :]]
        hi_t = [ring[0:STACK, 5, :], ring[0:STACK, 6, :]]

        pairs = [ctx.enter_context(nc.psum_tensor(f"pair{i}", [P, 2, T], F32)) for i in range(2)]
        singles = [ctx.enter_context(nc.psum_tensor(f"single{i}", [P, T], F32)) for i in range(2)]
        p_o = ctx.enter_context(nc.psum_tensor("p_o", [P, T], F32))
        p_m = ctx.enter_context(nc.psum_tensor("p_m", [P, T], F32))

        R = Ring(sig, "pair", pair_order(), 2)
        S1 = Ring(sig, "single", single_order(), 2)
        M = Ring(sig, "misc", misc_order(), 1)

        loads = [sem(f"load{i}") for i in range(4)]
        n_load = [0] * 4
        pool_ready = sem("pool_ready")
        POOL_SETUP = 11
        cols_full, cols_ready, exp_c, silu_ready = (sem(n) for n in ("cols_full", "cols_ready", "exp_c", "silu_ready"))
        mod_full, mod_ready, weights_ready = (sem(n) for n in ("mod_full", "mod_ready", "weights_ready"))
        setup_step = sem("setup_step")
        vec_step = sig("vec_step", V_STEPS)
        silu_b_ready = sig("silu_b_ready", 2)
        xn_ready = sig("xn_ready", 5)
        rot_ready = sig("rot_ready", 2)
        rope_done = sig("rope_done", 2)
        rope_q = sig("rope_q", 1)
        rope_k = sig("rope_k", 1)
        hi_ready = sig("hi_ready", 2 + 4 * NG)
        q_split = sig("q_split", 2 * NG)
        head_rows = [sem(f"head_rows{g}") for g in range(NG)]
        HEAD_ROWS = 16 * 2 * GH
        k_masked = sig("k_masked", 1)
        k_masked_pool = sig("k_masked_pool", GH * (NG - 1))
        m_split = sig("m_split", 2 * NG)
        m_rows = [sem(f"m_rows{g}") for g in range(NG)]
        M_ROWS = 16 * 2
        pv_done = sig("pv_done", 2 * NQ)
        oT_ready = sig("oT_ready", 2 * NG)
        logits_ready = sig("logits_ready", 2)
        rt_exp = sig("rt_exp", 2)
        gate_ready = sig("gate_ready", 2)
        x_ready = sig("x_ready", 4)
        stored = sem("stored")

        block = ctx.enter_context(nc.Block())

        def r32(ap):
            return ap.bitcast(F32R)

        def apart(eng):
            eng.nop(nofuse=True)

        def slot(g, j=0):
            return g % SETS * GH + j

        def column(L, j, b):
            return modT[:, L, j, bass.ds(b, 1)]

        def last_st(eng, b, L, n):
            S1.wait(eng, b, ("ST", L, n - 1))
            S1.wait(eng, b, ("ST", L, n))

        @block.sync
        def _(sp):
            def load(i, dst, src):
                sp.dma_start(dst, src).then_inc(loads[i], 16)
                n_load[i] += 16

            load(0, cst[:, :], a["const"])
            small = [(R_B0, a["L0_ffn_rb1"].rearrange("e (c p) -> (e c) p", p=P)),
                     (R_B0 + 2 * E0, a["L0_ffn_sb1"].rearrange("e (c p) -> (e c) p", p=P)),
                     (R_B1, a["L1_ffn_b1"].rearrange("e (c p) -> (e c) p", p=P)),
                     (R_LNG, a["L1_ffn_ln_g"].rearrange("(a d) -> a d", a=1)),
                     (R_LNB, a["L1_ffn_ln_b"].rearrange("(a d) -> a d", a=1)),
                     (R_C, a["L0_c"]), (R_C + NB, a["L1_c"])]
            for r, src in small:
                load(0, rows[r:r + src.shape[0], :], src)
            for L in range(2):
                load(0, w_mod[:, L, :, :], a[f"L{L}_wmod"].rearrange("d (j n) -> d j n", j=6))
            load(0, x[:, 0, :, :], a["L0_attn_x"][0].rearrange("(t p) d -> p t d", p=P))
            for dst, name in ((w_kvd, "W_kv_down"), (w_q, "W_q"), (w_kup, "W_k_up"), (w_vup, "W_v_up"), (w_o, "W_o")):
                load(1, dst[:, :], a[f"L0_attn_{name}"])
            load(1, w_rr[:, 0, :], a["L0_attn_W_q_rope"])
            load(1, w_rr[:, 1, :], a["L0_attn_W_k_rope"])
            sp.wait_ge(pool_ready, 2)
            G, GI, GO = a["L1_attn_w_qkv"].shape
            for g in range(G):
                load(1, w_qkv[GI * g:GI * (g + 1), GO * g:GO * (g + 1)], a["L1_attn_w_qkv"][g])
                load(1, w_proj[GI * g:GI * (g + 1), GI * g:GI * (g + 1)], a["L1_attn_w_proj"][g])
            load(1, b_proj[:, :], a["L1_attn_b_proj"].partition_broadcast(P))
            for L, (rw, rb) in enumerate((("L0_ffn_gW", "L0_ffn_gb"), ("L1_ffn_Wr", "L1_ffn_br"))):
                load(1, w_rt[L][:, :], a[rw])
                load(1, b_rt[L][:, :], a[rb].partition_broadcast(P))
            load(1, b_2[0][0:E0, :], a["L0_ffn_rb2"])
            load(1, b_2[0][E0:E0 + 1, :], a["L0_ffn_sb2"])
            load(1, b_2[1][:, :], a["L1_ffn_b2"])
            load(2, w1[0][:, 0:2 * E0, :].rearrange("d (e c) f -> d e (c f)", e=E0), a["L0_ffn_rW1"].rearrange("e d f -> d e f"))
            load(2, w1[0][:, 2 * E0:, :].rearrange("d c f -> d (c f)"), a["L0_ffn_sW1"][0])
            load(2, w2[0][:, 0:2 * E0, :], a["L0_ffn_rW2"].rearrange("e (c p) d -> p (e c) d", p=P))
            load(2, w2[0][:, 2 * E0:, :], a["L0_ffn_sW2"][0].rearrange("(c p) d -> p c d", p=P))
            load(3, w1[1][:, :, :].rearrange("d (e c) f -> d e (c f)", e=E1), a["L1_ffn_W1"].rearrange("e d f -> d e f"))
            load(3, w2[1][:, :, :], a["L1_ffn_W2"].rearrange("e (c p) d -> p (e c) d", p=P))
            for b in range(1, NB):
                load(3, x[:, b, :, :], a["L0_attn_x"][b].rearrange("(t p) d -> p t d", p=P))

            def m_dma(b, g):
                M.wait_taken(sp, b, ("mt", 0, g))
                for part in range(2):
                    sp.dma_start(q_op[K0 - 2 + part:K0 - 1 + part, slot(g):slot(g) + GH, :],
                                 mT[GH * NT * part:GH * NT * (part + 1), :]).then_inc(m_rows[g], 16)

            with sp.Fori(0, NB) as b:
                for g in range(NG):
                    if g >= SETS:
                        last_st(sp, b, 0, 16 * (g - SETS) + 15)
                    else:
                        S1.wait_full_before(sp, b)
                    for w, dst in enumerate((q_op, k_op)):
                        if w == 0:
                            q_split.wait(sp, b, g + 1)
                        else:
                            R.wait_taken(sp, b, ("heads", 0, g))
                        for j in range(GH):
                            sp.dma_start(dst[ROPE:ROPE + NOPE, slot(g, j), :],
                                         stk[NOPE * j:NOPE * (j + 1), 2 * w + g % 2, :]).then_inc(head_rows[g], 16)
                    if g == 2:
                        m_dma(b, 0)
                        m_dma(b, 1)
                m_dma(b, 2)
                m_dma(b, 3)
                x_ready.wait(sp, b)
                sp.dma_start(out[bass.ds(b, 1), :, :].rearrange("a (t p) d -> p (a t) d", p=P),
                             x[:, bass.ds(b, 1), :, :].rearrange("p a t d -> p (a t) d")).then_inc(stored, 16)
            sp.wait_ge(stored, 16 * NB)

        @block.gpsimd
        def _(pool):
            constant = [(w_qkv[:, :], 0.0), (w_proj[:, :], 0.0), (vaug[:, :, :, :], 0.0), (vaug[:, :, :, HD:HD + 1], 1.0),
                        (mrow1[:, :, :], 0.0), (stk[ROPE:P, :, :], 1.0), (k_op[ROPE:P, :, :], 1.0), (gate[:, :, :], 1.0),
                        (pw[:, :, :], -1.0), (topk[0][:, :, :], -1.0), (topk[1][:, :, :], -1.0)]
            assert len(constant) == POOL_SETUP
            for n, (dst, value) in enumerate(constant):
                pool.memset(dst, value).then_inc(pool_ready, 1)
                pool.wait_ge(pool_ready, n + 1)
            pool.wait_ge(loads[0], n_load[0])
            for s in signals.values():
                pool.sem_inc(s.sem, 1)
            pool.sem_inc(m_rows[NG - 1], 1)
            with pool.Fori(0, NB) as b:
                for g in range(1, NG):
                    R.wait_taken(pool, b, ("heads", 1, g))
                    if g >= SETS:
                        last_st(pool, b, 1, 16 * (g - SETS) + 15)
                    else:
                        last_st(pool, b, 0, NQ * GH - 1)
                    apart(pool)
                    for j in range(GH):
                        k_masked_pool.by(pool.tensor_scalar(r32(k_op[0:K1, slot(g, j), :]), stk[0:K1, g, :],
                                                            cst[0:K1, C_HM + j:C_HM + j + 1], None, ALU.mult))

        @block.scalar
        def _(act):
            act.wait_ge(cols_ready, 1)
            act.activation(silu[:, 1, :], cols[:, R_C:R_C + 2 * NB], ACT.Exp, scale=-1.0).then_inc(exp_c, 1)
            act.wait_ge(mod_ready, 1)
            act.wait_ge(loads[0], n_load[0])

            def high(src, rows_n, n, w):
                hi_ready.by(act.activation(r32(hi_t[w][0:rows_n, :]), src, ACT.Copy,
                                           scale=cst[0:rows_n, C_SG + 2 * n:C_SG + 2 * n + 1]))

            def out_rows(b, L, g):
                pv_done.wait(act, b, L * NQ + NT * (g + 1))
                if L == 0 and g == 0:
                    M.full[0].wait_before(act, b)
                else:
                    M.wait(act, b, ("ot", L, g - 1) if g else ("proj", 0))
                oT_ready.by(act.activation(oT[:, :], p_o[:, :], ACT.Copy))

            with act.Fori(0, NB) as b:
                for L in range(2):
                    s = R.wait(act, b, ("ln1", L))
                    if L == 0:
                        S1.wait_full_before(act, b)
                    else:
                        S1.wait(act, b, ("Y", 0, E0))
                    R.take(("ln1", L), act.activation(hT[:, :], pairs[s][:, 0, :], ACT.Identity,
                                                      bias=column(L, 0, b), scale=column(L, 1, b)))
                    if L == 0:
                        s = R.wait(act, b, "ckv")
                        R.take("ckv", act.activation(ckvT[:, :], pairs[s][:, 0, :], ACT.Copy))
                        for w in range(2):
                            rot_ready.wait(act, b, w + 1)
                            high(rot, ROPE, (SG_QR, SG_KR)[w], w)
                        rope_done.wait(act, b)
                    for g in range(NG):
                        s = R.wait(act, b, ("heads", L, g))
                        for w in range(2):
                            if g == 0:
                                pass
                            elif w == 0:
                                q_split.wait(act, b, L * NG + g)
                            else:
                                R.wait_taken(act, b, ("heads", L, g - 1))
                            high(pairs[s][0:STACK, w, :], STACK, ((SG_QN, SG_KN), (SG_Q1, SG_K1))[L][w], w)
                        if L == 0 and g == 0:
                            rope_k.by(act.activation(r32(k_op[0:ROPE, :, :]),
                                                     rope_op[1].unsqueeze(1).broadcast_to([ROPE, SETS * GH, T]), ACT.Copy))
                    s = R.wait(act, b, ("v", L))
                    pv_done.wait(act, b, L * NQ)
                    R.take(("v", L), act.activation(vaug[:, :, :, 0:HD],
                                                    pairs[s][:, 0, :].rearrange("p (t h d) -> p t h d", t=NT, d=HD), ACT.Copy))
                    for q in range(NQ):
                        g, kc = q // NT, q % NT
                        lo = P * kc if L == 0 else 0
                        for j in range(GH):
                            n = GH * q + j
                            s = S1.wait(act, b, ("ST", L, n))
                            if j == 0 and q >= 2:
                                pv_done.wait(act, b, L * NQ + q - 1)
                            S1.take(("ST", L, n), act.activation(ring[:, n % 8, lo:T], singles[s][:, lo:T], ACT.Exp))
                        if q >= NT and kc == 0:
                            out_rows(b, L, g - 1)
                    out_rows(b, L, NG - 1)
                    M.wait(act, b, ("on", L))
                    M.take(("on", L), act.activation(oT[:, :], p_m[:, :], ACT.Copy))
                    s = R.wait(act, b, ("ln2", L))
                    R.take(("ln2", L), act.activation(hT[:, :], pairs[s][:, 0, :], ACT.Identity,
                                                      bias=column(L, 3, b), scale=column(L, 4, b)))
                    if L == 1:
                        s = R.wait(act, b, "ln3")
                        R.take("ln3", act.activation(hT2[:, :], pairs[s][:, 0, :], ACT.Identity,
                                                     bias=cols[:, R_LNB:R_LNB + 1], scale=cols[:, R_LNG:R_LNG + 1]))
                    logits_ready.wait(act, b, L + 1)
                    rt_exp.by(act.activation(pr[:, :, 0:EX[L]], lg[:, :, 0:EX[L]], ACT.Exp))
                    for i in range(CU[L]):
                        s = R.wait(act, b, ("h", L, i))
                        if i >= 4:
                            S1.wait(act, b, ("Y", L, i - 4 if L == 0 else (i - 4) // 2))
                        for c in range(2):
                            col = (R_B0, R_B1)[L] + 2 * i + c
                            ins = act.activation(ring[:, 2 * (i % 4) + c, :], pairs[s][:, c, :],
                                                 (ACT.Gelu, ACT.Relu)[L], bias=cols[:, col:col + 1])
                        R.take(("h", L, i), ins)

        @block.tensor
        def _(pe):
            ident = cst[:, C_ID:C_ID + P]
            pe.wait_ge(loads[0], n_load[0])
            pe.transpose(p_m[:, 0:R_N], rows[:, :], cst[0:R_N, C_ID:C_ID + R_N]).then_inc(cols_full, 1)
            pe.wait_ge(silu_ready, 1)
            for L in range(2):
                for j in range(6):
                    n = (6 * L + j) * NB
                    ins = pe.matmul(p_o[:, n:n + NB], w_mod[:, L, j, :], silu[:, 0, NB * L:NB * (L + 1)], start=True, stop=True)
            ins.then_inc(mod_full, 1)
            pe.wait_ge(mod_ready, 1)
            pe.wait_ge(weights_ready, 1)

            def turn(dst, src, tiles=range(NT)):
                for t in tiles:
                    ins = pe.transpose(dst[:, P * t:P * (t + 1)], src[:, t, :], ident)
                return ins

            def condition(b, L):
                silu_b_ready.wait(pe, b, L + 1)
                M.open(pe, b, ("bc", L))
                M.fill(("bc", L), pe.matmul(p_m[:, :], silu_b[:, :], w_mod[:, L, 2:6, :].rearrange("p j n -> p (j n)"),
                                            start=True, stop=True))

            def normed(b, unit, k, src):
                xn_ready.wait(pe, b, k)
                s = R.open(pe, b, unit)
                R.fill(unit, turn(pairs[s][:, 0, :], src))

            def prepare(b, L):
                R.wait_taken(pe, b, ("ln1", L))
                if L == 0:
                    s = R.open(pe, b, "ckv")
                    R.fill("ckv", pe.matmul(pairs[s][:, 0, :], w_kvd[:, :], hT[:, :], start=True, stop=True))
                    for w in range(2):
                        s = R.open(pe, b, ("rope", w))
                        if w == 1:
                            R.wait_taken(pe, b, "ckv")
                        for v in range(2):
                            ins = pe.matmul(pairs[s][0:ROPE, v, :], w_rope[:, w, v, :], (hT, ckvT)[w][:, :], start=True, stop=True)
                        R.fill(("rope", w), ins)
                for g in range(NG):
                    s = R.open(pe, b, ("heads", L, g))
                    for w in range(2):
                        wgt = w_head1[:, w, g, :] if L else w_head0[:, w, GH * g:GH * (g + 1), :].rearrange("p h c -> p (h c)")
                        ins = pe.matmul(pairs[s][0:STACK, w, :], wgt, (ckvT if L == 0 and w else hT)[:, :], start=True, stop=True)
                    R.fill(("heads", L, g), ins)
                s = R.open(pe, b, ("v", L))
                for t in range(NT):
                    src = (ckvT, hT)[L][:, P * t:P * (t + 1)]
                    ins = pe.matmul(pairs[s][:, 0, P * t:P * (t + 1)], src, w_qkv[:, 2 * D:3 * D] if L else w_vup[:, :],
                                    start=True, stop=True)
                R.fill(("v", L), ins)

            def operands(b, L, g):
                if L == 0:
                    if g == 0:
                        rope_q.wait(pe, b)
                        rope_k.wait(pe, b)
                    pe.wait_ge(head_rows[g], b * HEAD_ROWS + HEAD_ROWS)
                elif g == 0:
                    k_masked.wait(pe, b)
                else:
                    k_masked_pool.wait(pe, b, GH * g)

            def scores(dst, L, lhs, rhs, lhs_lo, lo, hi, diagonal, kind):
                K = (K0, K1)[L]
                if kind == "S" and L == 0:
                    K = K0 - 2
                if kind == "S" and L == 1:
                    K = STACK
                ins = pe.matmul(dst[:, lo:hi], r32(lhs[0:K, lhs_lo:lhs_lo + P]), r32(rhs[0:K, lo:hi]), start=True, stop=L == 1)
                if L == 0:
                    ins = pe.matmul(dst[:, diagonal:diagonal + P], id_bf[:, :], mask_bf[:, 0 if kind == "S" else 1, :],
                                    start=False, stop=True)
                return ins

            def max_unit(b, L, n):
                g, p, qt = n // 8, n // 4 % 2, n % 4
                if n % 8 == 0:
                    operands(b, L, g)
                s = R.open(pe, b, ("S", L, n))
                hi = T if L else max(2 * P, P * (qt + 1))
                for i in range(2):
                    j = 2 * p + i
                    qs = q_op[:, g, :] if L else q_op[:, slot(g, j), :]
                    ins = scores(pairs[s][:, i, :], L, qs, k_op[:, slot(g, j), :], P * qt, 0, hi, P * qt, "S")
                R.fill(("S", L, n), ins)

            def max_turn(b, L, g):
                m_split.wait(pe, b, L * NG + g + 1)
                M.open(pe, b, ("mt", L, g))
                if L == 0:
                    ins = pe.transpose(p_m[0:2 * GH * NT, 0:P], mrow0[:, :, :, :].rearrange("p a j q -> p (a j q)"), ident)
                else:
                    for t in range(NT):
                        ins = pe.transpose(p_m[0:K1, P * t:P * (t + 1)], mrow1[:, t, :], ident)
                M.fill(("mt", L, g), ins)

            def exp_unit(b, L, n):
                g, kc, j = n // 16, n // 4 % 4, n % 4
                if n % 16 == 0:
                    if L == 0:
                        pe.wait_ge(m_rows[g], b * M_ROWS + M_ROWS + (g == NG - 1))
                    else:
                        M.wait_taken(pe, b, ("mt", 1, g))
                s = S1.open(pe, b, ("ST", L, n))
                qs = q_op[:, g, :] if L else q_op[:, slot(g, j), :]
                lo = 0 if L else min(2 * P, P * kc)
                S1.fill(("ST", L, n), scores(singles[s], L, k_op[:, slot(g, j), :], qs, P * kc, lo, T, P * kc, "ST"))

            def values(b, L, q):
                g, kc = q // NT, q % NT
                S1.wait_taken(pe, b, ("ST", L, GH * q + GH - 2))
                S1.wait_taken(pe, b, ("ST", L, GH * q + GH - 1))
                if kc == 0:
                    oT_ready.wait(pe, b, L * NG + g)
                if q == 0:
                    R.wait_taken(pe, b, ("v", L))
                lo = 0 if L else P * kc
                for j in range(GH):
                    ins = pe.matmul(p_o[32 * j:32 * (j + 1), lo:T], vaug[:, kc, GH * g + j, :], ring[:, (GH * q + j) % 8, lo:T],
                                    start=(kc == 0), stop=(kc == NT - 1))
                pv_done.by(ins)

            def out_turn(b, L, g):
                oT_ready.wait(pe, b, L * NG + g + 1)
                M.open(pe, b, ("ot", L, g))
                M.fill(("ot", L, g), turn(p_m, oT[:, :].rearrange("p (t n) -> p t n", t=NT)))

            def attention(b, L):
                for n in range(AHEAD[L]):
                    max_unit(b, L, n)
                    if n == 9:
                        max_turn(b, L, 0)
                for q in range(NQ):
                    s_units = s_of(L, q)
                    for j in range(GH):
                        exp_unit(b, L, GH * q + j)
                        if j == 1:
                            if q:
                                values(b, L, q - 1)
                            if q in MT_AT[L]:
                                max_turn(b, L, MT_AT[L][q])
                            if q in OT_AT:
                                out_turn(b, L, OT_AT[q])
                        if j >= 1 and s_units:
                            max_unit(b, L, s_units.pop(0))
                values(b, L, NQ - 1)
                out_turn(b, L, NG - 1)
                M.open(pe, b, ("on", L))
                M.wait_taken(pe, b, ("ot", L, NG - 1))
                M.fill(("on", L), turn(p_m, onorm))
                M.open(pe, b, ("proj", L))
                for t in range(NT):
                    ins = pe.matmul(p_m[:, P * t:P * (t + 1)], oT[:, P * t:P * (t + 1)], (w_o, w_proj)[L][:, :], start=True, stop=True)
                M.fill(("proj", L), ins)

            def hidden(b, L, i):
                s = R.open(pe, b, ("h", L, i))
                for c in range(2):
                    ins = pe.matmul(pairs[s][:, c, :], w1[L][:, 2 * i + c, :], (hT, hT2)[L][:, :], start=True, stop=True)
                R.fill(("h", L, i), ins)

            def expert_out(b, L, e):
                ch = chunks_of(L, e)
                if ch:
                    for i in sorted({c // 2 for c in ch}):
                        R.wait_taken(pe, b, ("h", L, i))
                s = S1.open(pe, b, ("Y", L, e))
                for t in range(NT):
                    ts = slice(P * t, P * (t + 1))
                    parts = [(ring[:, c % 8, ts], w2[L][:, c, :]) for c in ch]
                    if e == EX[L]:
                        parts.append((gateT[0:(E0 + 1, E1)[L], ts], b_2[L][:, :]))
                        if L == 0:
                            parts.append((hT[:, ts], ident))
                    for k, (lhs, rhs) in enumerate(parts):
                        ins = pe.matmul(singles[s][:, ts], lhs, rhs, start=(k == 0), stop=(k == len(parts) - 1))
                S1.fill(("Y", L, e), ins)

            def experts(b, L):
                R.wait_taken(pe, b, ("ln2", L))
                M.open(pe, b, ("lg", L))
                for t in range(NT):
                    ins = pe.matmul(p_m[:, 16 * t:16 * t + EX[L]], hT[:, P * t:P * (t + 1)], w_rt[L][:, :], start=True, stop=True)
                M.fill(("lg", L), ins)
                pe.wait_ge(loads[2 + L], n_load[2 + L])
                if L == 1:
                    normed(b, "ln3", 5, onorm)
                    R.wait_taken(pe, b, "ln3")
                done = 0
                for i in range(CU[L]):
                    hidden(b, L, i)
                    ready = i - 2 if L == 0 else (i - 1) // 2
                    if i == 3:
                        gate_ready.wait(pe, b, L + 1)
                        M.open(pe, b, ("gt", L))
                        for t in range(NT):
                            ins = pe.transpose(p_m[0:16, P * t:P * (t + 1)], gate[:, t, :], ident)
                        M.fill(("gt", L), ins)
                    while i >= 3 and done < ready:
                        expert_out(b, L, done)
                        done += 1
                M.wait_taken(pe, b, ("gt", L))
                while done <= EX[L]:
                    expert_out(b, L, done)
                    done += 1

            with pe.Fori(0, NB) as b:
                for L in range(2):
                    normed(b, ("ln1", L), (1, 3)[L], xn)
                    condition(b, L)
                    prepare(b, L)
                    attention(b, L)
                    normed(b, ("ln2", L), (2, 4)[L], xn)
                    experts(b, L)

        @block.vector
        def _(dve):
            n_setup = [0]

            def settle(ins):
                ins.then_inc(setup_step, 1)
                n_setup[0] += 1
                dve.wait_ge(setup_step, n_setup[0])

            dve.wait_ge(cols_full, 1)
            dve.tensor_copy(cols[:, :], p_m[:, 0:R_N]).then_inc(cols_ready, 1)
            dve.wait_ge(exp_c, 1)
            settle(dve.tensor_scalar(silu[:, 2, :], silu[:, 1, :], 1.0, None, ALU.add))
            settle(dve.reciprocal(silu[:, 1, :], silu[:, 2, :]))
            dve.wait_ge(cols_ready, 1)
            dve.tensor_tensor(silu[:, 0, :], silu[:, 1, :], cols[:, R_C:R_C + 2 * NB], ALU.mult).then_inc(silu_ready, 1)
            dve.tensor_copy(id_bf[:, :], cst[:, C_ID:C_ID + P])
            dve.tensor_copy(mask_bf[:, :, :], cst[:, C_MS:C_MS + 2 * P].rearrange("p (a n) -> p a n", a=2))
            dve.wait_ge(mod_full, 1)
            settle(dve.tensor_copy(modT[:, :, :, :].rearrange("p l j b -> p (l j b)"), p_o[:, 0:12 * NB]))
            dve.tensor_scalar(modT[:, :, 1, :], modT[:, :, 1, :], 1.0, None, ALU.add)
            dve.tensor_scalar(modT[:, :, 4, :], modT[:, :, 4, :], 1.0, None, ALU.add).then_inc(mod_ready, 1)
            dve.wait_ge(loads[1], n_load[1])
            for w in range(2):
                plain = w_rope[:, w, 0, :].rearrange("p (t r) -> p t r", t=TERMS)
                swap = w_rope[:, w, 1, :].rearrange("p (t r) -> p t r", t=TERMS)
                rr, half = w_rr[:, w, :].unsqueeze(1), DR // 2
                dve.tensor_copy(plain, rr.broadcast_to([P, TERMS, DR]))
                dve.tensor_copy(swap[:, :, 0:half], rr[:, :, half:DR].broadcast_to([P, TERMS, half]))
                dve.tensor_copy(swap[:, :, half:DR], rr[:, :, 0:half].broadcast_to([P, TERMS, half]))
                for t in range(TERMS):
                    dve.tensor_copy(w_head0[:, w, :, HD * t:HD * (t + 1)], (w_q, w_kup)[w][:, :].rearrange("p (h d) -> p h d", h=H))
                    ins = dve.tensor_copy(w_head1[:, w, :, GH * HD * t:GH * HD * (t + 1)],
                                          w_qkv[:, D * w:D * (w + 1)].rearrange("p (g n) -> p g n", g=NG))
            ins.then_inc(weights_ready, 1)
            dve.wait_ge(weights_ready, 1)
            dve.wait_ge(mod_ready, 1)
            dve.wait_ge(loads[0], n_load[0])
            dve.wait_ge(pool_ready, POOL_SETUP)

            def step(b, ins):
                vec_step.by(ins)
                vec_step.wait(dve, b, vec_step.made)

            def norm(b, src, dst):
                apart(dve)
                for t in range(NT):
                    ins = dve.bn_stats(stats[:, t, :], src(t))
                step(b, ins)
                apart(dve)
                for t in range(NT):
                    ins = dve.bn_aggr(mv[:, t, :], stats[:, t, :])
                step(b, ins)
                v, y, z = nwt[:, 0, :], nwt[:, 1, :], nwt[:, 2, :]
                step(b, dve.tensor_scalar(v, mv[:, :, 1], EPS, None, ALU.add))
                step(b, dve.tensor_scalar(y.bitcast(I32), v.bitcast(I32), -0.5, float(0x5F3759DF), ALU.mult, ALU.add))
                for _ in range(3):
                    step(b, dve.scalar_tensor_tensor(out=z, in0=y, scalar=-0.5, in1=y, op0=ALU.mult, op1=ALU.mult))
                    step(b, dve.tensor_tensor(z, z, v, ALU.mult))
                    step(b, dve.scalar_tensor_tensor(out=y, in0=z, scalar=1.5, in1=y, op0=ALU.add, op1=ALU.mult))
                for t in range(NT):
                    ins = dve.tensor_scalar(dst[:, t, :], src(t), mv[:, t, 0:1], nwt[:, 1, t:t + 1], ALU.subtract, ALU.mult)
                xn_ready.by(ins)

            def x_of(b):
                return lambda t: x[:, bass.ds(b, 1), t, :].rearrange("p a d -> p (a d)")

            def x_row(b):
                return x[:, bass.ds(b, 1), :, :].rearrange("p a t d -> p (a t) d")

            def over_tiles(ap):
                return ap.unsqueeze(1).broadcast_to([P, NT, D])

            def condition(b, L):
                silu_b_ready.by(dve.tensor_copy(silu_b[:, :], silu[:, 0, bass.ds(b + NB * L, 1)].broadcast_to([P, P])))

            def guards(b, L):
                M.wait(dve, b, ("bc", L))
                M.take(("bc", L), dve.tensor_copy(bc[L][:, :, :].rearrange("p j n -> p (j n)"), p_m[:, :]))
                M.wait_taken(dve, b, ("bc", L))
                g = bc[L][:, 0:4:3, :]
                step(b, dve.tensor_scalar(gsign[:, :, :], g, 0.0, 2.0, ALU.is_ge, ALU.mult))
                step(b, dve.scalar_tensor_tensor(out=g, in0=g, scalar=-1.0, in1=g, op0=ALU.mult, op1=ALU.max))
                step(b, dve.tensor_scalar(g, g, 0.25, None, ALU.max))
                step(b, dve.scalar_tensor_tensor(out=g, in0=gsign[:, :, :], scalar=-1.0, in1=g, op0=ALU.add, op1=ALU.mult))
                if L == 1:
                    step(b, dve.tensor_scalar(bc[1][:, 2, :], bc[1][:, 2, :], 1.0, None, ALU.add))

            def low(src, dst, rows_n, n, w):
                return dve.scalar_tensor_tensor(out=r32(dst), in0=src, scalar=cst[0:rows_n, C_SG + 2 * n + 1:C_SG + 2 * n + 2],
                                                in1=hi_t[w][0:rows_n, :], op0=ALU.mult, op1=ALU.add)

            def rope(b, w):
                s = R.wait(dve, b, ("rope", w))
                dve.tensor_tensor(rot_a, pairs[s][0:ROPE, 0, :], cst[0:ROPE, C_COS:C_COS + T], ALU.mult)
                R.take(("rope", w), dve.tensor_tensor(rot_b, pairs[s][0:ROPE, 1, :], cst[0:ROPE, C_SIN:C_SIN + T], ALU.mult))
                R.wait_taken(dve, b, ("rope", w))
                rot_ready.by(dve.tensor_tensor(rot, rot_a, rot_b, ALU.add))
                rot_ready.wait(dve, b, w + 1)
                hi_ready.wait(dve, b, w + 1)
                rope_done.by(low(rot, rope_op[w], ROPE, (SG_QR, SG_KR)[w], w))
                rope_done.wait(dve, b, w + 1)
                if w == 0:
                    S1.wait_full_before(dve, b)
                    rope_q.by(dve.tensor_copy(r32(q_op[0:ROPE, :, :]), rope_op[0].unsqueeze(1).broadcast_to([ROPE, SETS * GH, T])))

            def heads(b, L, g):
                s = R.wait(dve, b, ("heads", L, g))
                if L == 0:
                    if g < 2:
                        k_masked_pool.wait_before(dve, b)
                    else:
                        dve.wait_ge(head_rows[g - 2], b * HEAD_ROWS + HEAD_ROWS)
                elif g == 0:
                    for n in (2, 3):
                        dve.wait_ge(head_rows[n], b * HEAD_ROWS + HEAD_ROWS)
                    last_st(dve, b, 0, NQ * GH - 1)
                for w in range(2):
                    hi_ready.wait(dve, b, 2 + 2 * NG * L + 2 * g + w + 1)
                    dst = stk[0:STACK, 2 * w + g % 2, :] if L == 0 else (q_op, stk)[w][0:STACK, g, :]
                    ins = low(pairs[s][0:STACK, w, :], dst, STACK, ((SG_QN, SG_KN), (SG_Q1, SG_K1))[L][w], w)
                    q_split.by(ins) if w == 0 else R.take(("heads", L, g), ins)
                if L == 1 and g == 0:
                    R.wait_taken(dve, b, ("heads", 1, 0))
                    for j in range(GH):
                        ins = dve.tensor_scalar(r32(k_op[0:K1, slot(0, j), :]), stk[0:K1, 0, :],
                                                cst[0:K1, C_HM + j:C_HM + j + 1], None, ALU.mult)
                    k_masked.by(ins)

            def max_unit(b, L, n):
                g, p, qt = n // 8, n // 4 % 2, n % 4
                s = R.wait(dve, b, ("S", L, n))
                hi = T if L else P * (qt + 1)
                R.take(("S", L, n), dve.tensor_reduce(mneg[:, g % 2, qt, 2 * p:2 * p + 2], pairs[s][:, :, 0:hi],
                                                      axis=AX.X, op=ALU.max, negate=True))

            def max_split(b, L, g):
                for n in (8 * g + 6, 8 * g + 7):
                    R.wait_taken(dve, b, ("S", L, n))
                m = mneg[:, g % 2, :, :]
                if L == 0:
                    hi, lo, m = mrow0[:, 0, :, :], mrow0[:, 1, :, :], m.rearrange("p q j -> p j q")
                else:
                    hi, lo = mrow1[:, :, STACK:STACK + GH], mrow1[:, :, STACK + GH:K1]
                step(b, dve.tensor_copy(r32(hi), m))
                m_split.by(dve.tensor_tensor(r32(lo), m, hi, ALU.subtract))

            def max_rows(b, L, g):
                M.wait(dve, b, ("mt", L, g))
                if L == 0:
                    if g:
                        dve.wait_ge(m_rows[g - 1], b * M_ROWS + M_ROWS)
                    else:
                        dve.wait_ge(m_rows[NG - 1], b * M_ROWS + 1)
                    ins = dve.tensor_copy(r32(mT[:, :]), p_m[0:2 * GH * NT, 0:P])
                else:
                    ins = dve.tensor_copy(r32(q_op[STACK:K1, g, :]), p_m[STACK:K1, :])
                M.take(("mt", L, g), ins)

            def normalise(b, L, g):
                M.wait(dve, b, ("ot", L, g))
                o = p_m[:, :].rearrange("p (q j c) -> p q j c", q=NT, j=GH)
                step(b, dve.reciprocal(rsum[:, :, :], o[:, :, :, HD]))
                dst = onorm[:, :, :].rearrange("p q (g j d) -> p q g j d", g=NG, j=GH)[:, :, g, :, :]
                M.take(("ot", L, g), dve.tensor_tensor(dst, o[:, :, :, 0:HD], rsum[:, :, :].unsqueeze(3).broadcast_to([P, NT, GH, HD]), ALU.mult))

            def attention(b, L):
                for n in range(AHEAD[L]):
                    max_unit(b, L, n)
                    if n % 8 == 7:
                        max_split(b, L, n // 8)
                    if n == 9:
                        max_rows(b, L, 0)
                for q in range(NQ):
                    if q in MT_AT[L]:
                        max_rows(b, L, MT_AT[L][q])
                    if q in OT_AT:
                        normalise(b, L, OT_AT[q])
                    for n in s_of(L, q):
                        max_unit(b, L, n)
                        if n % 8 == 7:
                            max_split(b, L, n // 8)
                normalise(b, L, NG - 1)
                M.wait(dve, b, ("proj", L))
                pm = p_m[:, :].rearrange("p (t d) -> p t d", t=NT)
                M.take(("proj", L), dve.tensor_tensor(acc[:, :, :], pm, over_tiles(bc[0][:, 0, :] if L == 0 else b_proj[:, :]),
                                                      ALU.mult if L == 0 else ALU.add))
                M.wait_taken(dve, b, ("proj", L))
                if L == 1:
                    step(b, dve.tensor_tensor(acc[:, :, :], acc[:, :, :], over_tiles(bc[1][:, 0, :]), ALU.mult))
                x_ready.by(dve.tensor_tensor(x_row(b), x_row(b), acc[:, :, :], ALU.add))
                x_ready.wait(dve, b, 2 * L + 1)

            def routing(b, L):
                E, k = EX[L], (TOP, 1)[L]
                lo = 16 - E
                M.wait(dve, b, ("lg", L))
                lgv, rm = lg[:, :, 0:E], rmax[:, 0, :]

                def wide(ap):
                    return ap.unsqueeze(2).broadcast_to([P, NT, E])

                M.take(("lg", L), dve.tensor_tensor(lgv, p_m[:, 0:16 * NT].rearrange("p (t e) -> p t e", t=NT)[:, :, 0:E],
                                                    b_rt[L][:, :].unsqueeze(1).broadcast_to([P, NT, E]), ALU.add))
                M.wait_taken(dve, b, ("lg", L))
                step(b, dve.tensor_reduce(rm, lgv, axis=AX.X, op=ALU.max))
                logits_ready.by(dve.tensor_tensor(lgv, lgv, wide(rm), ALU.subtract))
                rt_exp.wait(dve, b, L + 1)
                step(b, dve.tensor_reduce(rmax[:, 1, :], pr[:, :, 0:E], axis=AX.X, op=ALU.add))
                step(b, dve.reciprocal(rm, rmax[:, 1, :]))
                step(b, dve.tensor_tensor(pw[:, :, lo:16], pr[:, :, 0:E], wide(rm), ALU.mult))
                apart(dve)
                for t in range(NT):
                    ins = dve.max(top[:, t, :], pw[:, t, lo:24])
                step(b, ins)
                step(b, dve.tensor_copy(topk[L][:, :, 0:k], top[:, :, 0:k]))
                apart(dve)
                for t in range(NT):
                    ins = dve.match_replace(pr[:, t, lo:24], topk[L][:, t, :], pw[:, t, lo:24], -2.0)
                step(b, ins)
                gate_ready.by(dve.scalar_tensor_tensor(out=gate[:, :, 0:E], in0=pr[:, :, lo:16], scalar=-2.0, in1=pw[:, :, lo:16],
                                                       op0=ALU.is_equal, op1=ALU.mult))
                gate_ready.wait(dve, b, L + 1)

            def experts(b, L):
                E = EX[L]
                if L == 1:
                    xn_ready.wait(dve, b, 4)
                    step(b, dve.tensor_tensor(acc[:, :, :], xn[:, :, :], over_tiles(bc[1][:, 2, :]), ALU.mult))
                    step(b, dve.tensor_tensor(acc[:, :, :], acc[:, :, :], over_tiles(bc[1][:, 1, :]), ALU.add))
                    norm(b, lambda t: acc[:, t, :], onorm)
                    xn_ready.wait(dve, b, 5)
                routing(b, L)
                M.wait(dve, b, ("gt", L))
                M.take(("gt", L), dve.tensor_copy(gateT[:, :], p_m[0:16, :]))
                for e in range(E):
                    s = S1.wait(dve, b, ("Y", L, e))
                    if e:
                        S1.wait_taken(dve, b, ("Y", L, e - 1))
                    for t in range(NT):
                        y, gt = singles[s][:, P * t:P * (t + 1)], gate[:, t, e:e + 1]
                        if e == 0:
                            ins = dve.tensor_scalar(acc[:, t, :], y, gt, None, ALU.mult)
                        else:
                            ins = dve.scalar_tensor_tensor(out=acc[:, t, :], in0=y, scalar=gt, in1=acc[:, t, :], op0=ALU.mult, op1=ALU.add)
                    S1.take(("Y", L, e), ins)
                s = S1.wait(dve, b, ("Y", L, E))
                S1.wait_taken(dve, b, ("Y", L, E - 1))
                S1.take(("Y", L, E), dve.tensor_tensor(acc[:, :, :].rearrange("p t d -> p (t d)"), singles[s][:, :],
                                                       acc[:, :, :].rearrange("p t d -> p (t d)"), ALU.add))
                S1.wait_taken(dve, b, ("Y", L, E))
                step(b, dve.tensor_tensor(acc[:, :, :], acc[:, :, :], over_tiles(bc[L][:, 3, :]), ALU.mult))
                x_ready.by(dve.tensor_tensor(x_row(b), x_row(b), acc[:, :, :], ALU.add))
                x_ready.wait(dve, b, 2 * L + 2)

            with dve.Fori(0, NB) as b:
                for L in range(2):
                    condition(b, L)
                    norm(b, x_of(b), xn)
                    guards(b, L)
                    if L == 0:
                        for w in range(2):
                            rope(b, w)
                    for g in range(NG):
                        heads(b, L, g)
                    attention(b, L)
                    norm(b, x_of(b), xn)
                    experts(b, L)

        for name, s in signals.items():
            assert s.made == s.per, (name, s.made, s.per)


_INS = ['L0_attn_x', 'L0_attn_W_kv_down', 'L0_attn_W_k_up', 'L0_attn_W_v_up', 'L0_attn_W_q', 'L0_attn_W_q_rope',
        'L0_attn_W_k_rope', 'L0_attn_W_o', 'L0_ffn_sW1', 'L0_ffn_sb1', 'L0_ffn_sW2', 'L0_ffn_sb2', 'L0_ffn_rW1',
        'L0_ffn_rb1', 'L0_ffn_rW2', 'L0_ffn_rb2', 'L0_ffn_gW', 'L0_ffn_gb', 'L0_c', 'L0_wmod', 'L1_attn_w_qkv',
        'L1_attn_w_proj', 'L1_attn_b_proj', 'L1_ffn_Wr', 'L1_ffn_br', 'L1_ffn_ln_g', 'L1_ffn_ln_b', 'L1_ffn_W1',
        'L1_ffn_b1', 'L1_ffn_W2', 'L1_ffn_b2', 'L1_c', 'L1_wmod']


def kernel(**inputs):
    import concourse.bacc as _bacc
    from concourse.bass_utils import run_bass_kernel_spmd as _run

    nc = _bacc.Bacc("TRN2", target_bir_lowering=False, num_devices=1)
    arrays, args = {}, {}
    for name in _INS:
        arrays[f"in_{name}_dram"] = v = np.ascontiguousarray(inputs[name])
        args[name] = nc.dram_tensor(f"in_{name}_dram", v.shape, mybir.dt.from_np(v.dtype), kind="ExternalInput").ap()
    arrays["const_dram"] = c = constants()
    args["const"] = nc.dram_tensor("const_dram", c.shape, F32, kind="ExternalInput").ap()
    out = nc.dram_tensor("out_dram", (NB, T, D), F32, kind="ExternalOutput").ap()
    build(nc, args, out)
    r = _run(nc, [arrays], core_ids=[0])
    return r.results[0]["out_dram"]
```

```python
from contextlib import ExitStack

import concourse.bass as bass
import numpy as np
from concourse import mybir

F32 = mybir.dt.float32
F32R = mybir.dt.float32r
BF16 = mybir.dt.bfloat16
I32 = mybir.dt.int32
ALU = mybir.AluOpType
ACT = mybir.ActivationFunctionType
AX = mybir.AxisListType

P = 128
NB, T, D = 4, 512, 128
NT = T // P
H, HD = 16, 8
DR = 32
NG, GH = 4, 4
E0, E1 = 15, 8
TOP = 3
C0, C1 = 2 * E0 + 4, 4 * E1
TERMS = 3
STACK = TERMS * GH * HD
ROPE = TERMS * DR
NOPE = TERMS * HD
K0 = ROPE + NOPE + 2
K1 = STACK + 2 * GH
SETS = 3
SCALE0 = 1.0 / float(np.sqrt(HD + DR))
SCALE1 = float(HD) ** -0.5
MASKED = -1e30
EPS = 1e-5

C_ID, C_MS, C_MT, C_HM, C_SG = 0, P, 2 * P, 3 * P, 3 * P + GH
C_SEL = C_SG + 12
C_COS = C_SEL + 16
C_SIN = C_COS + T
C_N = C_SIN + T
SG_Q1, SG_K1, SG_QN, SG_KN, SG_QR, SG_KR = range(6)
R_B0, R_B1, R_LNG, R_LNB, R_BP, R_C = 0, C0, C0 + C1, C0 + C1 + 1, C0 + C1 + 2, C0 + C1 + 3
R_N = R_C + 2 * NB
PREP_STEPS = [13, 13]
MAIN_STEPS = [31, 43]


def constants():
    c = np.zeros((P, C_N), np.float32)
    p = np.arange(P)
    c[:, C_ID:C_ID + P] = np.eye(P)
    c[:, C_MS:C_MS + P] = np.where(p[None, :] > p[:, None], MASKED, 0)
    c[:, C_MT:C_MT + P] = np.where(p[:, None] > p[None, :], MASKED, 0)
    c[:, C_SEL:C_SEL + 16] = (p[:, None] < 32) & (p[:, None] % 16 == np.arange(16)[None, :])
    for j in range(GH):
        own = ((p < STACK) & (p % (GH * HD) // HD == j)) | (p == STACK + j) | (p == STACK + GH + j)
        c[:, C_HM + j] = own

    def split(n, low, scale):
        c[:, C_SG + 2 * n] = np.where(low, -scale, scale)
        c[:, C_SG + 2 * n + 1] = np.where(low, scale, 0)

    split(SG_Q1, p // (GH * HD) == 2, SCALE1)
    split(SG_K1, p // (GH * HD) == 1, 1.0)
    split(SG_QN, p % NOPE // HD == 2, SCALE0)
    split(SG_KN, p % NOPE // HD == 1, 1.0)
    split(SG_QR, p // DR == 2, SCALE0)
    split(SG_KR, p // DR == 1, 1.0)
    inv = (np.float32(1.0) / np.float32(10000.0) ** (np.arange(0, DR, 2, dtype=np.float32) / np.float32(DR))).astype(np.float32)
    f = np.outer(np.arange(T, dtype=np.float32), inv).astype(np.float32).T
    c[:ROPE, C_COS:C_COS + T] = np.tile(np.cos(f), (2 * TERMS, 1))
    c[:ROPE, C_SIN:C_SIN + T] = np.tile(np.concatenate([-np.sin(f), np.sin(f)]), (TERMS, 1))
    return c


class Row:

    def __init__(self, b, off=0):
        self.b, self.off = b, off

    def index(self):
        return self.b + self.off

    def at(self, per, k):
        return self.b * per + (self.off * per + k)

    def before(self):
        return None if isinstance(self.b, int) and self.b + self.off == 0 else Row(self.b, self.off - 1)


class Signal:

    def __init__(self, sem, per):
        self.sem, self.per, self.made = sem, per, 0

    def _wait(self, eng, value):
        eng.wait_ge(self.sem, value)
        if eng.engine == mybir.EngineType.SP:
            eng.nop(nofuse=True)

    def by(self, ins):
        ins.then_inc(self.sem, 1)
        self.made += 1
        return ins

    def wait(self, eng, row, k=None):
        self._wait(eng, row.at(self.per, (self.per if k is None else k) + 1))

    def wait_before(self, eng, row):
        self._wait(eng, row.at(self.per, 1))


class Ring:

    def __init__(self, sig, name, order, slots):
        self.where, n = {}, [0] * slots
        for i, unit in enumerate(order):
            assert unit not in self.where, unit
            self.where[unit] = (i % slots, n[i % slots])
            n[i % slots] += 1
        self.full = [sig(f"{name}{s}_full", n[s]) for s in range(slots)]
        self.taken = [sig(f"{name}{s}_taken", n[s]) for s in range(slots)]

    def open(self, eng, row, unit):
        s, k = self.where[unit]
        self.taken[s].wait(eng, row, k)
        return s

    def fill(self, unit, ins):
        self.full[self.where[unit][0]].by(ins)

    def wait(self, eng, row, unit):
        s, k = self.where[unit]
        self.full[s].wait(eng, row, k + 1)
        return s

    def take(self, unit, ins):
        self.taken[self.where[unit][0]].by(ins)

    def wait_taken(self, eng, row, unit):
        s, k = self.where[unit]
        self.taken[s].wait(eng, row, k + 1)

    def wait_full_before(self, eng, row):
        for f in self.full:
            f.wait_before(eng, row)


NS = NG * (GH // 2) * NT
NQ = NG * NT
AHEAD = [16, 10]
S_PACE = [[2, 2, 2, 2, 0, 0, 3, 3, 2, 0, 0, 0, 0, 0, 0, 0],
          [3, 3, 0, 0, 3, 3, 2, 0, 3, 3, 2, 0, 0, 0, 0, 0]]
MT_AT = [{1: 1, 5: 2, 10: 3}, {3: 1, 7: 2, 11: 3}]
OT_AT = {6: 0, 9: 1, 13: 2}
CU = [C0 // 2, C1 // 2]
EX = [E0, E1]
UNITS = [1, 2]
DEPTH = 3
SPLIT = 2
STAGES, STAGE = 3, 8
PIECES = [[(which, lo, min(lo + STAGE, hi)) for which in range(2) for lo0, hi in ((0, 2 * E0), (2 * E0, C0))
           for lo in range(lo0, hi, STAGE)],
          [(which, lo, lo + STAGE) for which in range(2) for lo in range(0, C1, STAGE)]]

HEADS = [("heads", g, w) for g in range(NG) for w in range(2)]
PARTS = [["norm", "ln1", "ckv", ("rope", 0, 0), ("rope", 0, 1), ("rope", 1, 0), ("rope", 1, 1)] + HEADS + ["v"],
         ["norm", "ln1"] + HEADS + ["v"]]
PREP_AT = [{("q", 13): PARTS[0][0:1], "out": PARTS[0][1:2], "on": PARTS[0][2:3], "proj": PARTS[0][3:4], "lg": PARTS[0][4:5],
            "gt": PARTS[0][5:6]},
           {("q", 13): PARTS[1][0:1], "out": PARTS[1][1:2], "lg": PARTS[1][2:3], "gt": PARTS[1][3:4]}]
for _L in range(2):
    for _n, _part in enumerate(PARTS[_L][(6, 4)[_L]:]):
        PREP_AT[_L][("u", 2 + _n)] = [_part]
ROPE_K = {3 + n: n for n in range(1, SETS * GH)}


def s_of(L, q):
    first = AHEAD[L] + sum(S_PACE[L][:q])
    return list(range(first, first + S_PACE[L][q]))


def pair_order(L):
    return [("S", n) for n in range(NS)] + [("h", i) for i in range(CU[L])]


def misc_order(L):
    out = [("mt", 0)]
    for q in range(NQ):
        if q in MT_AT[L]:
            out.append(("mt", MT_AT[L][q]))
        if q in OT_AT:
            out.append(("ot", OT_AT[q]))
    return out + [("ot", NG - 1), "on", "proj", "xa", "ln2", "lg"] + ([], ["hb", "ln3"])[L] + ["gt", "xy"]


def expert_of(L, i):
    return (i if i < E0 else None) if L == 0 else i // 2


def build(nc, a, out):
    ctx = ExitStack()
    with ctx:
        def sb(name, shape, dt=F32):
            return ctx.enter_context(nc.sbuf_tensor(name, shape, dt))

        def sem(name):
            return ctx.enter_context(nc.semaphore(name))

        signals = {}

        def sig(name, per):
            signals[name] = Signal(sem(name), per)
            return signals[name]

        def layers(name, per0, per1):
            return [sig(f"{name}_{L}", per) if per else None for L, per in enumerate((per0, per1))]

        cst = sb("cst", [P, C_N])
        rows = sb("rows", [R_N, P])
        cols = sb("cols", [P, R_N])
        w_kvd, w_vup, w_o = (sb(n, [P, P]) for n in ("w_kvd", "w_vup", "w_o"))
        w_rope = sb("w_rope", [P, 2, 2, ROPE])
        w_head = sb("w_head", [P, 2, NG, STACK])
        w_qkv = sb("w_qkv", [P, 3 * D])
        w_proj = sb("w_proj", [P, D])
        w12 = sb("w12", [P, 2, 2, C0, P])
        w_rt = [sb("w_rt0", [P, E0]), sb("w_rt1", [P, E1])]
        b_rt = [sb("b_rt0", [P, E0]), sb("b_rt1", [P, E1])]
        b_2 = sb("b_2", [P, 2, D])
        sel = sb("sel", [P, 16])
        id_bf = sb("id_bf", [P, P], BF16)
        mask_bf = sb("mask_bf", [P, 2, P], BF16)
        silu = sb("silu", [P, 3, 2 * NB])
        modT = sb("modT", [P, 2, 6, NB])
        guard = sb("guard", [P, 2, 2, NB])
        x = sb("x", [P, NB, NT, D])
        stats = sb("stats", [P, NT, 6])
        mv = sb("mv", [P, NT, 2])
        nwt = sb("nwt", [P, 3, NT])
        xn = sb("xn", [P, NT, D])
        hT = sb("hT", [P, T])
        ckvT = sb("ckvT", [P, T])
        q_op = sb("q_op", [P, SETS * GH, T])
        k_op = sb("k_op", [P, SETS * GH, T])
        stk = sb("stk", [P, 4, T])
        vaug = sb("vaug", [P, NT, H, HD + 1])
        ring = sb("ring", [P, 8, T])
        hid_hi = sb("hid_hi", [P, SPLIT, 2, T])
        hid_lo = sb("hid_lo", [P, SPLIT, 2, T])
        mneg = sb("mneg", [P, 2, NT, GH])
        mrow0 = sb("mrow0", [P, 2, GH, NT])
        mrow1 = sb("mrow1", [P, NT, K1])
        mT = sb("mT", [2 * GH * NT, P])
        oT = sb("oT", [P, T])
        rsum = sb("rsum", [P, NT, GH])
        onorm = sb("onorm", [P, NT, D])
        hF = sb("hF", [P, T])
        h_hi = sb("h_hi", [P, T])
        h_lo = sb("h_lo", [P, T])
        lg = sb("lg", [P, NT, 16])
        pw = sb("pw", [P, NT, 24])
        pr = sb("pr", [P, NT, 24])
        rmax = sb("rmax", [P, 2, NT])
        top = sb("top", [P, NT, 8])
        topk = [sb("topk0", [P, NT, 8]), sb("topk1", [P, NT, 8])]
        gate = sb("gate", [P, NT, 16])
        gate2 = sb("gate2", [P, NT, 32])
        gateT = sb("gateT", [P, T])
        tmp = [ring[0:ROPE, 6, :], ring[0:ROPE, 7, :], oT[0:ROPE, :]]
        stage = ring[:, 0:6, :].rearrange("p s t -> p (s t)").rearrange("p (k c n) -> p k c n", k=STAGES, n=P)
        w_mod = x[:, 1:, :, :].rearrange("p b t d -> p (b t d)").rearrange("p (l j n) -> p l j n", l=2, j=6)
        raw = onorm[:, :, :].rearrange("p t d -> p (t d)")
        w_q, w_kup, w_rr = raw[:, 0:D], raw[:, D:2 * D], raw[:, 2 * D:2 * D + 2 * DR].rearrange("p (w r) -> p w r", w=2)

        pairs = [ctx.enter_context(nc.psum_tensor(f"pair{i}", [P, 2, T], F32)) for i in range(2)]
        singles = [ctx.enter_context(nc.psum_tensor(f"single{i}", [P, T], F32)) for i in range(2)]
        p_o = ctx.enter_context(nc.psum_tensor("p_o", [P, T], F32))
        p_m = ctx.enter_context(nc.psum_tensor("p_m", [P, T], F32))
        gates = [singles[1], p_m]
        p_x = singles[0]

        R = [Ring(sig, f"pair_{L}_", pair_order(L), 2) for L in range(2)]
        S1 = [Ring(sig, f"single_{L}_", [("ST", n) for n in range(NQ * GH)], 2) for L in range(2)]
        M = [Ring(sig, f"misc_{L}_", misc_order(L), 1) for L in range(2)]
        X = [Ring(sig, f"prep_{L}_", [p for p in PARTS[L] if p != "norm"], 1) for L in range(2)]

        loads = [sem(f"load{i}") for i in range(4)]
        n_load = [0] * 4
        pool_ready = sem("pool_ready")
        cols_full, cols_ready, exp_c, silu_ready = (sem(n) for n in ("cols_full", "cols_ready", "exp_c", "silu_ready"))
        mod_full, mod_ready, weights_ready = (sem(n) for n in ("mod_full", "mod_ready", "weights_ready"))
        setup_step = sem("setup_step")
        staged = [sem(f"staged{k}") for k in range(STAGES)]
        w_hi, w_lo = sem("w_hi"), sem("w_lo")
        prep_step = layers("prep_step", *PREP_STEPS)
        main_step = layers("main_step", *MAIN_STEPS)
        xn_ready = layers("xn_ready", 1, 1)
        on_ready = layers("on_ready", 1, 1)
        rot_ready = layers("rot_ready", 2, 0)
        rope_done = layers("rope_done", 2, 0)
        rope_q = layers("rope_q", 1, 0)
        rope_k = layers("rope_k", len(ROPE_K), 0)
        hi_ready = layers("hi_ready", 2 + 2 * NG, 2 * NG)
        head_rows = [sem(f"head_rows{g}") for g in range(NG)]
        HEAD_ROWS = 16 * 2 * GH
        k_masked = layers("k_masked", 0, GH * NG)
        m_split = layers("m_split", NG, NG)
        m_rows = [sem(f"m_rows{g}") for g in range(NG)]
        M_ROWS = 16 * 2
        pv_done = layers("pv_done", NQ, NQ)
        oT_ready = layers("oT_ready", NG, NG)
        logits_ready = layers("logits_ready", 1, 1)
        rt_exp = layers("rt_exp", 1, 1)
        gate_ready = layers("gate_ready", 1, 1)
        spread = layers("spread", *EX)
        h_lo_ready = layers("h_lo_ready", 1, 1)
        gated = layers("gated", E0, C1 // 2)
        g_hi = layers("g_hi", *CU)
        g_lo = layers("g_lo", *CU)
        y_step = layers("y_step", *CU)
        y_taken = layers("y_taken", 1, 1)
        stored = sem("stored")

        block = ctx.enter_context(nc.Block())

        def r32(ap):
            return ap.bitcast(F32R)

        def apart(eng):
            eng.nop(nofuse=True)

        def slot(g, j=0):
            return g % SETS * GH + j

        def column(L, j, row):
            return modT[:, L, j, bass.ds(row.index(), 1)]

        def last_st(eng, row, L, n):
            S1[L].wait(eng, row, ("ST", n - 1))
            S1[L].wait(eng, row, ("ST", n))

        LAST = Row(NB - 1)

        def layer_start(eng, L):
            if L == 1:
                M[0].wait_taken(eng, LAST, "xy")

        def first_piece(L):
            return L * len(PIECES[0])

        def piece(L, n):
            which, lo, hi = PIECES[L][n]
            return (first_piece(L) + n) % STAGES, hi - lo, w12[:, which, 0, lo:hi, :], w12[:, which, 1, lo:hi, :]

        def pieces_after(L, i):
            n = i - (4, 1)[L]
            last = i == len(PARTS[L]) - 1
            return range(max(n, 0), len(PIECES[L])) if last else [n] if 0 <= n < len(PIECES[L]) else []

        def parts_at(L, point):
            return PREP_AT[L].get(point, ())

        @block.sync
        def _(sp):
            def load(i, dst, src):
                sp.dma_start(dst, src).then_inc(loads[i], 16)
                n_load[i] += 16

            load(0, cst[:, :], a["const"])
            small = [(R_B0, a["L0_ffn_rb1"].rearrange("e (c p) -> (e c) p", p=P)),
                     (R_B0 + 2 * E0, a["L0_ffn_sb1"].rearrange("e (c p) -> (e c) p", p=P)),
                     (R_B1, a["L1_ffn_b1"].rearrange("e (c p) -> (e c) p", p=P)),
                     (R_LNG, a["L1_ffn_ln_g"].rearrange("(a d) -> a d", a=1)),
                     (R_LNB, a["L1_ffn_ln_b"].rearrange("(a d) -> a d", a=1)),
                     (R_BP, a["L1_attn_b_proj"].rearrange("(a d) -> a d", a=1)),
                     (R_C, a["L0_c"]), (R_C + NB, a["L1_c"])]
            for r, src in small:
                load(0, rows[r:r + src.shape[0], :], src)
            for L in range(2):
                load(0, w_mod[:, L, :, :], a[f"L{L}_wmod"].rearrange("d (j n) -> d j n", j=6))
            load(0, x[:, 0, :, :], a["L0_attn_x"][0].rearrange("(t p) d -> p t d", p=P))
            for dst, name in ((w_kvd[:, :], "W_kv_down"), (w_q, "W_q"), (w_kup, "W_k_up"), (w_vup[:, :], "W_v_up"),
                              (w_o[:, :], "W_o"), (w_rr[:, 0, :], "W_q_rope"), (w_rr[:, 1, :], "W_k_rope")):
                load(1, dst, a[f"L0_attn_{name}"])

            def expert_loads(L):
                for n, (which, lo, hi) in enumerate(PIECES[L]):
                    if first_piece(L) + n >= STAGES:
                        sp.wait_ge(w_lo, first_piece(L) + n + 1 - STAGES)
                    k, per = (first_piece(L) + n) % STAGES, (2, 4)[L]
                    dst = stage[:, k, 0:hi - lo, :]
                    if lo == 2 * E0 and L == 0:
                        src = a["L0_ffn_sW1"][0] if which == 0 else a["L0_ffn_sW2"][0].rearrange("(c p) d -> p c d", p=P)
                        dst = dst.rearrange("p c n -> p (c n)") if which == 0 else dst
                    elif which == 0:
                        src = a[("L0_ffn_rW1", "L1_ffn_W1")[L]][lo // per:hi // per].rearrange("e d f -> d e f")
                        dst = dst.rearrange("p (e c) n -> p e (c n)", c=per)
                    else:
                        src = a[("L0_ffn_rW2", "L1_ffn_W2")[L]][lo // per:hi // per].rearrange("e (c p) d -> p (e c) d", p=P)
                    sp.dma_start(dst, src).then_inc(staged[k], 16)

            expert_loads(0)
            def m_dma(row, g):
                M[0].wait_taken(sp, row, ("mt", g))
                for part in range(2):
                    sp.dma_start(q_op[K0 - 2 + part:K0 - 1 + part, slot(g):slot(g) + GH, :],
                                 mT[GH * NT * part:GH * NT * (part + 1), :]).then_inc(m_rows[g], 16)

            def head_dma(row, g):
                if g >= SETS:
                    last_st(sp, row, 0, 16 * (g - SETS) + 15)
                else:
                    S1[0].wait_full_before(sp, row)
                for w, dst in enumerate((q_op, k_op)):
                    X[0].wait_taken(sp, row, ("heads", g, w))
                    for j in range(GH):
                        sp.dma_start(dst[ROPE:ROPE + NOPE, slot(g, j), :],
                                     stk[NOPE * j:NOPE * (j + 1), 2 * w + g % 2, :]).then_inc(head_rows[g], 16)

            def main(row):
                m_dma(row, 0)
                m_dma(row, 1)
                head_dma(row, SETS)
                m_dma(row, 2)
                m_dma(row, 3)

            for g in range(SETS):
                head_dma(Row(0), g)
            sp.wait_ge(pool_ready, 3)
            for r in (0, 16):
                load(2, b_2[r:r + E0, 0, :], a["L0_ffn_rb2"])
                load(2, b_2[r + E0:r + E0 + 1, 0, :], a["L0_ffn_sb2"])
                load(2, b_2[r:r + E1, 1, :], a["L1_ffn_b2"])
            for L, (rw, rb) in enumerate((("L0_ffn_gW", "L0_ffn_gb"), ("L1_ffn_Wr", "L1_ffn_br"))):
                load(2, w_rt[L][:, :], a[rw])
                load(2, b_rt[L][:, :], a[rb].partition_broadcast(P))
            N_G, GI, GO = a["L1_attn_w_qkv"].shape
            for g in range(N_G):
                load(2, w_qkv[GI * g:GI * (g + 1), GO * g:GO * (g + 1)], a["L1_attn_w_qkv"][g])
                load(2, w_proj[GI * g:GI * (g + 1), GI * g:GI * (g + 1)], a["L1_attn_w_proj"][g])
            sp.wait_ge(mod_full, 1)
            for b in range(1, NB):
                load(3, x[:, b, :, :], a["L0_attn_x"][b].rearrange("(t p) d -> p t d", p=P))
            with sp.Fori(0, NB - 1) as b:
                main(Row(b))
                for g in range(SETS):
                    head_dma(Row(b, 1), g)
            main(LAST)
            layer_start(sp, 1)
            expert_loads(1)
            with sp.Fori(0, NB) as b:
                M[1].wait_taken(sp, Row(b), "xy")
                sp.dma_start(out[bass.ds(b, 1), :, :].rearrange("a (t p) d -> p (a t) d", p=P),
                             x[:, bass.ds(b, 1), :, :].rearrange("p a t d -> p (a t) d")).then_inc(stored, 16)
            sp.wait_ge(stored, 16 * NB)

        constant = [(w_qkv[:, :], 0.0), (w_proj[:, :], 0.0), (b_2[:, :, :], 0.0),
                    (vaug[:, :, :, HD:HD + 1], 1.0), (mrow1[:, :, :], 0.0), (stk[ROPE:P, :, :], 1.0), (k_op[ROPE:P, :, :], 1.0),
                    (gate[:, :, :], 1.0), (pw[:, :, :], -1.0), (topk[0][:, :, :], -1.0), (topk[1][:, :, :], -1.0), (gateT[:, :], 0.0)]
        POOL_SETUP = len(constant)

        @block.gpsimd
        def _(pool):
            for n, (dst, value) in enumerate(constant):
                pool.memset(dst, value).then_inc(pool_ready, 1)
                pool.wait_ge(pool_ready, n + 1)
            for s in signals.values():
                pool.sem_inc(s.sem, 1)
            pool.sem_inc(m_rows[NG - 1], 1)
            pool.wait_ge(loads[0], n_load[0])

            def spread_rope(row):
                rope_done[0].wait(pool, row, 1)
                S1[0].wait_full_before(pool, row)
                apart(pool)
                rope_q[0].by(pool.tensor_copy(r32(q_op[0:ROPE, 1:, :]), q_op[0:ROPE, 0:1, :].broadcast_to([ROPE, SETS * GH - 1, T])))

            def mask(row, g):
                X[1].wait_taken(pool, row, ("heads", g, 1))
                if g >= SETS:
                    last_st(pool, row, 1, 16 * (g - SETS) + 15)
                else:
                    S1[1].wait_full_before(pool, row)
                apart(pool)
                for j in range(GH):
                    k_masked[1].by(pool.tensor_scalar(r32(k_op[0:K1, slot(g, j), :]), stk[0:K1, g, :],
                                                      cst[0:K1, C_HM + j:C_HM + j + 1], None, ALU.mult))

            spread_rope(Row(0))
            with pool.Fori(0, NB - 1) as b:
                spread_rope(Row(b, 1))
            layer_start(pool, 1)
            for g in range(SETS):
                mask(Row(0), g)
            with pool.Fori(0, NB - 1) as b:
                mask(Row(b), SETS)
                for g in range(SETS):
                    mask(Row(b, 1), g)
            mask(LAST, SETS)

        @block.scalar
        def _(act):
            act.wait_ge(cols_ready, 1)
            act.activation(silu[:, 1, :], cols[:, R_C:R_C + 2 * NB], ACT.Exp, scale=-1.0).then_inc(exp_c, 1)
            act.wait_ge(mod_ready, 1)
            act.wait_ge(loads[0], n_load[0])

            def high(L, dst, src, n):
                hi_ready[L].by(act.activation(r32(dst), src, ACT.Copy,
                                              scale=cst[0:dst.shape[0], C_SG + 2 * n:C_SG + 2 * n + 1]))

            def prep(row, L, part):
                if row is None or part == "norm":
                    return
                if part == "ln1":
                    X[L].wait(act, row, part)
                    X[L].full[0].wait_before(act, row)
                    X[L].take(part, act.activation(hT[:, :], p_x[:, :], ACT.Identity, bias=column(L, 0, row), scale=column(L, 1, row)))
                elif part == "ckv":
                    X[L].wait(act, row, part)
                    X[L].take(part, act.activation(ckvT[:, :], p_x[:, :], ACT.Copy))
                elif part == "v":
                    X[L].wait(act, row, part)
                    pv_done[L].wait_before(act, row)
                    X[L].take(part, act.activation(vaug[:, :, :, 0:HD], p_x[:, :].rearrange("p (t h d) -> p t h d", t=NT, d=HD), ACT.Copy))
                elif part[0] == "rope":
                    _, w, v = part
                    if v == 1:
                        rot_ready[0].wait(act, row, w + 1)
                        if w == 0:
                            if row.before():
                                M[0].wait(act, row.before(), "proj")
                        else:
                            rope_done[0].wait(act, row, 1)
                        high(0, tmp[2], tmp[0], (SG_QR, SG_KR)[w])
                else:
                    _, g, w = part
                    X[L].wait(act, row, part)
                    if g:
                        X[L].wait_taken(act, row, ("heads", g - 1, w))
                    elif L == 0:
                        rope_done[0].wait(act, row)
                    else:
                        pv_done[1].wait_before(act, row)
                    high(L, tmp[w], p_x[0:STACK, :], ((SG_QN, SG_KN), (SG_Q1, SG_K1))[L][w])

            def spread_rope(row, i):
                if row is None or i not in ROPE_K:
                    return
                n = ROPE_K[i]
                rope_done[0].wait(act, row)
                S1[0].wait_full_before(act, row)
                rope_k[0].by(act.activation(r32(k_op[0:ROPE, n, :]), k_op[0:ROPE, 0, :], ACT.Copy))

            def out_rows(row, L, g):
                pv_done[L].wait(act, row, NT * (g + 1))
                if g:
                    M[L].wait(act, row, ("ot", g - 1))
                else:
                    M[L].full[0].wait_before(act, row)
                oT_ready[L].by(act.activation(oT[:, :], p_o[:, :], ACT.Copy))

            def row_work(row, L, nxt):
                def prep_at(point):
                    for part in parts_at(L, point):
                        prep(nxt, L, part)

                y_step[L].wait_before(act, row)
                X[L].taken[0].wait(act, row)
                for q in range(NQ):
                    g, kc = q // NT, q % NT
                    lo = P * kc if L == 0 else 0
                    for j in range(GH):
                        n = GH * q + j
                        s = S1[L].wait(act, row, ("ST", n))
                        if j == 0 and q >= 2:
                            pv_done[L].wait(act, row, q - 1)
                        S1[L].take(("ST", n), act.activation(ring[:, n % 8, lo:T], singles[s][:, lo:T], ACT.Exp))
                    if q >= NT and kc == 0:
                        out_rows(row, L, g - 1)
                    prep_at(("q", q))
                out_rows(row, L, NG - 1)
                prep_at("out")
                M[L].wait(act, row, "on")
                M[L].take("on", act.activation(oT[:, :], p_m[:, :], ACT.Copy))
                prep_at("on")
                prep_at("proj")
                M[L].wait(act, row, "ln2")
                shift, scale = column(L, 3, row), column(L, 4, row)
                if L == 0:
                    act.activation(r32(h_hi[:, :]), p_m[:, :], ACT.Identity, bias=shift, scale=scale)
                    ins = act.activation(hF[:, :], p_m[:, :], ACT.Identity, bias=shift, scale=scale)
                    M[L].take("ln2", ins)
                else:
                    M[L].take("ln2", act.activation(hF[:, :], p_m[:, :], ACT.Identity, bias=shift, scale=scale))
                    M[L].wait(act, row, "ln3")
                    shift, scale = cols[:, R_LNB:R_LNB + 1], cols[:, R_LNG:R_LNG + 1]
                    act.activation(r32(h_hi[:, :]), p_m[:, :], ACT.Identity, bias=shift, scale=scale)
                    M[L].take("ln3", act.activation(hF[:, :], p_m[:, :], ACT.Identity, bias=shift, scale=scale))
                logits_ready[L].wait(act, row)
                rt_exp[L].by(act.activation(pr[:, :, 0:EX[L]], lg[:, :, 0:EX[L]], ACT.Exp))
                prep_at("lg")
                prep_at("gt")

                def hidden_hi(i):
                    if expert_of(L, i) is None:
                        R[L].wait_taken(act, row, ("h", i))
                    else:
                        gated[L].wait(act, row, i + 1)
                    if i >= SPLIT:
                        y_step[L].wait(act, row, i - SPLIT + 1)
                    k = i % DEPTH
                    g_hi[L].by(act.activation(r32(hid_hi[:, i % SPLIT, :, :]), ring[:, 2 * k:2 * k + 2, :], ACT.Copy))

                for i in range(CU[L]):
                    s = R[L].wait(act, row, ("h", i))
                    if i >= DEPTH:
                        g_lo[L].wait(act, row, i - DEPTH + 1)
                    for c in range(2):
                        col = (R_B0, R_B1)[L] + 2 * i + c
                        ins = act.activation(ring[:, 2 * (i % DEPTH) + c, :], pairs[s][:, c, :],
                                             (ACT.Gelu, ACT.Relu)[L], bias=cols[:, col:col + 1])
                    R[L].take(("h", i), ins)
                    if i:
                        hidden_hi(i - 1)
                    prep_at(("u", i))
                    if L == 0:
                        spread_rope(nxt, i)
                hidden_hi(CU[L] - 1)

            for L in range(2):
                layer_start(act, L)
                for i, part in enumerate(PARTS[L]):
                    prep(Row(0), L, part)
                    if L == 0 and i >= 7:
                        for n in range(i - 3, i - 2 if i < len(PARTS[0]) - 1 else max(ROPE_K) + 1):
                            spread_rope(Row(0), n)
                    for n in pieces_after(L, i):
                        k, chunks, hi, _ = piece(L, n)
                        act.wait_ge(staged[k], 16 * ((first_piece(L) + n) // STAGES + 1))
                        act.activation(r32(hi), stage[:, k, 0:chunks, :], ACT.Copy).then_inc(w_hi, 1)
                with act.Fori(0, NB - 1) as b:
                    row_work(Row(b), L, Row(b, 1))
                row_work(LAST, L, None)

        @block.tensor
        def _(pe):
            ident = cst[:, C_ID:C_ID + P]
            pe.wait_ge(loads[0], n_load[0])
            pe.transpose(p_m[:, 0:R_N], rows[:, :], cst[0:R_N, C_ID:C_ID + R_N]).then_inc(cols_full, 1)
            pe.wait_ge(silu_ready, 1)
            for L in range(2):
                for j in range(6):
                    n = (6 * L + j) * NB
                    ins = pe.matmul(p_o[:, n:n + NB], w_mod[:, L, j, :], silu[:, 0, NB * L:NB * (L + 1)], start=True, stop=True)
            ins.then_inc(mod_full, 1)
            pe.wait_ge(mod_ready, 1)

            def turn(dst, src):
                for t in range(NT):
                    ins = pe.transpose(dst[:, P * t:P * (t + 1)], src[:, t, :], ident)
                return ins

            def tiles(ap):
                return ap.rearrange("p (t n) -> p t n", t=NT)

            def prep(row, L, part):
                if row is None or part == "norm":
                    return
                if part == "ln1":
                    xn_ready[L].wait(pe, row)
                    S1[L].taken[0].wait_before(pe, row)
                X[L].open(pe, row, part)
                if part == "ln1":
                    ins = turn(p_x, xn)
                elif part == "ckv":
                    ins = pe.matmul(p_x[:, :], w_kvd[:, :], hT[:, :], start=True, stop=True)
                elif part == "v":
                    for t in range(NT):
                        src = (ckvT, hT)[L][:, P * t:P * (t + 1)]
                        ins = pe.matmul(p_x[:, P * t:P * (t + 1)], src, w_qkv[:, 2 * D:3 * D] if L else w_vup[:, :],
                                        start=True, stop=True)
                elif part[0] == "rope":
                    _, w, v = part
                    ins = pe.matmul(p_x[0:ROPE, :], w_rope[:, w, v, :], (hT, ckvT)[w][:, :], start=True, stop=True)
                else:
                    _, g, w = part
                    ins = pe.matmul(p_x[0:STACK, :], w_head[:, w, g, :], (ckvT if L == 0 and w else hT)[:, :], start=True, stop=True)
                X[L].fill(part, ins)

            def operands(row, L, g):
                if L == 0:
                    if g == 0:
                        rope_q[0].wait(pe, row)
                        rope_k[0].wait(pe, row)
                    pe.wait_ge(head_rows[g], row.at(HEAD_ROWS, HEAD_ROWS))
                else:
                    k_masked[1].wait(pe, row, GH * (g + 1))

            def scores(dst, L, lhs, rhs, lhs_lo, lo, hi, diagonal, kind):
                K = (K0, K1)[L]
                if kind == "S":
                    K = (K0 - 2, STACK)[L]
                ins = pe.matmul(dst[:, lo:hi], r32(lhs[0:K, lhs_lo:lhs_lo + P]), r32(rhs[0:K, lo:hi]), start=True, stop=L == 1)
                if L == 0:
                    ins = pe.matmul(dst[:, diagonal:diagonal + P], id_bf[:, :], mask_bf[:, 0 if kind == "S" else 1, :],
                                    start=False, stop=True)
                return ins

            def max_unit(row, L, n):
                g, p, qt = n // 8, n // 4 % 2, n % 4
                if n % 8 == 0:
                    operands(row, L, g)
                s = R[L].open(pe, row, ("S", n))
                hi = T if L else max(2 * P, P * (qt + 1))
                for i in range(2):
                    j = 2 * p + i
                    qs = q_op[:, g, :] if L else q_op[:, slot(g, j), :]
                    ins = scores(pairs[s][:, i, :], L, qs, k_op[:, slot(g, j), :], P * qt, 0, hi, P * qt, "S")
                R[L].fill(("S", n), ins)

            def max_turn(row, L, g):
                m_split[L].wait(pe, row, g + 1)
                M[L].open(pe, row, ("mt", g))
                if L == 0:
                    ins = pe.transpose(p_m[0:2 * GH * NT, 0:P], mrow0[:, :, :, :].rearrange("p a j q -> p (a j q)"), ident)
                else:
                    for t in range(NT):
                        ins = pe.transpose(p_m[0:K1, P * t:P * (t + 1)], mrow1[:, t, :], ident)
                M[L].fill(("mt", g), ins)

            def exp_unit(row, L, n):
                g, kc, j = n // 16, n // 4 % 4, n % 4
                if n % 16 == 0:
                    if L == 0:
                        pe.wait_ge(m_rows[g], row.at(M_ROWS, M_ROWS + (g == NG - 1)))
                    else:
                        M[1].wait_taken(pe, row, ("mt", g))
                if n == 0:
                    X[L].taken[0].wait(pe, row)
                elif n == 1:
                    gated[L].wait_before(pe, row)
                s = S1[L].open(pe, row, ("ST", n))
                qs = q_op[:, g, :] if L else q_op[:, slot(g, j), :]
                lo = 0 if L else min(2 * P, P * kc)
                S1[L].fill(("ST", n), scores(singles[s], L, k_op[:, slot(g, j), :], qs, P * kc, lo, T, P * kc, "ST"))

            def values(row, L, q):
                g, kc = q // NT, q % NT
                S1[L].wait_taken(pe, row, ("ST", GH * q + GH - 2))
                S1[L].wait_taken(pe, row, ("ST", GH * q + GH - 1))
                if q == 0:
                    y_taken[L].wait_before(pe, row)
                elif kc == 0:
                    oT_ready[L].wait(pe, row, g)
                lo = 0 if L else P * kc
                for j in range(GH):
                    ins = pe.matmul(p_o[32 * j:32 * j + HD + 1, lo:T], vaug[:, kc, GH * g + j, :], ring[:, (GH * q + j) % 8, lo:T],
                                    start=(kc == 0), stop=(kc == NT - 1))
                pv_done[L].by(ins)

            def out_turn(row, L, g):
                oT_ready[L].wait(pe, row, g + 1)
                M[L].open(pe, row, ("ot", g))
                M[L].fill(("ot", g), turn(p_m, tiles(oT[:, :])))

            def row_work(row, L, nxt):
                def prep_at(point):
                    for part in parts_at(L, point):
                        prep(nxt, L, part)

                for n in range(AHEAD[L]):
                    max_unit(row, L, n)
                    if n == 9:
                        max_turn(row, L, 0)
                for q in range(NQ):
                    s_units = s_of(L, q)
                    for j in range(GH):
                        exp_unit(row, L, GH * q + j)
                        if j == 1:
                            if q:
                                values(row, L, q - 1)
                            if q in MT_AT[L]:
                                max_turn(row, L, MT_AT[L][q])
                            if q in OT_AT:
                                out_turn(row, L, OT_AT[q])
                        if j >= 1 and s_units:
                            max_unit(row, L, s_units.pop(0))
                values(row, L, NQ - 1)
                prep_at("out")
                out_turn(row, L, NG - 1)
                M[L].open(pe, row, "on")
                M[L].fill("on", turn(p_m, onorm))
                prep_at("on")
                M[L].open(pe, row, "proj")
                M[L].fill("proj", pe.matmul(p_m[:, :], (w_o, w_proj)[L][:, :], oT[:, :], start=True, stop=True))
                prep_at("proj")
                M[L].open(pe, row, "xa")
                M[L].fill("xa", turn(p_m, tiles(hF[:, :])))
                on_ready[L].wait(pe, row)
                M[L].open(pe, row, "ln2")
                M[L].fill("ln2", turn(p_m, onorm))
                M[L].open(pe, row, "lg")
                for t in range(NT):
                    ins = pe.matmul(p_m[:, 16 * t:16 * t + EX[L]], hF[:, P * t:P * (t + 1)], w_rt[L][:, :], start=True, stop=True)
                M[L].fill("lg", ins)
                if L == 1:
                    M[1].open(pe, row, "hb")
                    M[1].fill("hb", turn(p_m, tiles(hF[:, :])))
                prep_at("lg")
                if L == 1:
                    M[1].open(pe, row, "ln3")
                    M[1].fill("ln3", turn(p_m, onorm))

                def hidden(i):
                    s = R[L].open(pe, row, ("h", i))
                    for c in range(2):
                        n = 2 * i + c
                        hi, lo = (r32(w12[:, 0, part, n, :]) for part in range(2))
                        pe.matmul(pairs[s][:, c, :], hi, r32(h_hi[:, :]), start=True, stop=False)
                        pe.matmul(pairs[s][:, c, :], hi, r32(h_lo[:, :]), start=False, stop=False)
                        ins = pe.matmul(pairs[s][:, c, :], lo, r32(h_hi[:, :]), start=False, stop=True)
                    R[L].fill(("h", i), ins)

                def spread_gate(e):
                    if e == 0:
                        S1[L].wait_taken(pe, row, ("ST", NQ * GH - 1))
                    if e >= 2:
                        gated[L].wait(pe, row, UNITS[L] * (e - 1))
                    spread[L].by(pe.matmul(gates[e % 2][:, :], r32(sel[:, e:e + 1].broadcast_to([P, P])), r32(gateT[:, :]),
                                           start=True, stop=True))

                def second(i):
                    g_lo[L].wait(pe, row, i + 1)
                    k = i % SPLIT
                    for c in range(2):
                        n = 2 * i + c
                        hi, lo = (r32(w12[:, 1, part, n, :]) for part in range(2))
                        rest = hid_lo[:, k, c, :]
                        pe.matmul(p_o[:, :], hi, r32(hid_hi[:, k, c, :]), start=False, stop=False)
                        pe.matmul(p_o[:, :], hi, r32(rest), start=False, stop=False)
                        ins = pe.matmul(p_o[:, :], lo, r32(hid_hi[:, k, c, :]), start=False, stop=(n == 2 * CU[L] - 1))
                    y_step[L].by(ins)

                pe.wait_ge(w_lo, first_piece(L) + len(PIECES[L]))
                h_lo_ready[L].wait(pe, row)
                for i in range(CU[L]):
                    hidden(i)
                    if i == 1:
                        prep_at("gt")
                        gate_ready[L].wait(pe, row)
                        M[L].open(pe, row, "gt")
                        for t in range(NT):
                            ins = pe.transpose(p_m[0:32, P * t:P * (t + 1)], gate2[:, t, :], ident)
                        M[L].fill("gt", ins)
                        M[L].wait_taken(pe, row, "gt")
                        spread_gate(0)
                        spread_gate(1)
                        if L == 0:
                            pe.wait_ge(loads[2], n_load[2])
                        oT_ready[L].wait(pe, row)
                        pe.matmul(p_o[:, :], b_2[:, L, :], gateT[:, :], start=True, stop=False)
                    if i >= DEPTH:
                        second(i - DEPTH)
                    e = i + 1 if L == 0 else (i + 2) // 2
                    if i >= 1 and 2 <= e < EX[L] and (L == 0 or i % 2 == 0):
                        spread_gate(e)
                    prep_at(("u", i))
                for i in range(CU[L] - DEPTH, CU[L]):
                    second(i)
                y_taken[L].wait(pe, row)
                gated[L].wait(pe, row)
                M[L].open(pe, row, "xy")
                M[L].fill("xy", turn(p_m, tiles(hF[:, :])))

            for L in range(2):
                layer_start(pe, L)
                pe.wait_ge(weights_ready, L + 1)
                for part in PARTS[L]:
                    prep(Row(0), L, part)
                with pe.Fori(0, NB - 1) as b:
                    row_work(Row(b), L, Row(b, 1))
                row_work(LAST, L, None)

        @block.vector
        def _(dve):
            n_setup = [0]

            def settle(ins):
                ins.then_inc(setup_step, 1)
                n_setup[0] += 1
                dve.wait_ge(setup_step, n_setup[0])

            dve.wait_ge(cols_full, 1)
            dve.tensor_copy(cols[:, :], p_m[:, 0:R_N]).then_inc(cols_ready, 1)
            dve.wait_ge(exp_c, 1)
            settle(dve.tensor_scalar(silu[:, 2, :], silu[:, 1, :], 1.0, None, ALU.add))
            settle(dve.reciprocal(silu[:, 1, :], silu[:, 2, :]))
            dve.wait_ge(cols_ready, 1)
            dve.tensor_tensor(silu[:, 0, :], silu[:, 1, :], cols[:, R_C:R_C + 2 * NB], ALU.mult).then_inc(silu_ready, 1)
            dve.tensor_copy(id_bf[:, :], cst[:, C_ID:C_ID + P])
            dve.tensor_copy(r32(sel[:, :]), cst[:, C_SEL:C_SEL + 16])
            dve.tensor_copy(mask_bf[:, :, :], cst[:, C_MS:C_MS + 2 * P].rearrange("p (a n) -> p a n", a=2))
            dve.wait_ge(mod_full, 1)
            settle(dve.tensor_copy(modT[:, :, :, :].rearrange("p l j b -> p (l j b)"), p_o[:, 0:12 * NB]))
            dve.memset(p_o[:, :], 0.0)
            gg = modT[:, :, 2:6:3, :]
            settle(dve.tensor_scalar(guard[:, :, :, :], gg, 0.0, 2.0, ALU.is_ge, ALU.mult))
            settle(dve.scalar_tensor_tensor(out=gg, in0=gg, scalar=-1.0, in1=gg, op0=ALU.mult, op1=ALU.max))
            settle(dve.tensor_scalar(gg, gg, 0.25, None, ALU.max))
            settle(dve.scalar_tensor_tensor(out=gg, in0=guard[:, :, :, :], scalar=-1.0, in1=gg, op0=ALU.add, op1=ALU.mult))
            dve.tensor_scalar(modT[:, :, 1, :], modT[:, :, 1, :], 1.0, None, ALU.add)
            dve.tensor_scalar(modT[:, :, 4, :], modT[:, :, 4, :], 1.0, None, ALU.add).then_inc(mod_ready, 1)
            dve.wait_ge(mod_ready, 1)
            dve.wait_ge(loads[0], n_load[0])

            def head_weights(L):
                dve.wait_ge(loads[1], n_load[1])
                for w in range(2):
                    for t in range(TERMS):
                        if L == 0:
                            src = (w_q, w_kup)[w].rearrange("p (g h d) -> p g h d", g=NG, d=HD)
                            dst = w_head[:, w, :, :].rearrange("p g (h c) -> p g h c", c=NOPE)[:, :, :, HD * t:HD * (t + 1)]
                            for g in range(NG):
                                ins = dve.tensor_copy(dst[:, g, :, :], src[:, g, :, :])
                        else:
                            ins = dve.tensor_copy(w_head[:, w, :, GH * HD * t:GH * HD * (t + 1)],
                                                  w_qkv[:, D * w:D * (w + 1)].rearrange("p (g n) -> p g n", g=NG))
                    if L == 0:
                        plain = w_rope[:, w, 0, :].rearrange("p (t r) -> p t r", t=TERMS)
                        swap = w_rope[:, w, 1, :].rearrange("p (t r) -> p t r", t=TERMS)
                        rr, half = w_rr[:, w, :].unsqueeze(1), DR // 2
                        dve.tensor_copy(plain, rr.broadcast_to([P, TERMS, DR]))
                        dve.tensor_copy(swap[:, :, 0:half], rr[:, :, half:DR].broadcast_to([P, TERMS, half]))
                        ins = dve.tensor_copy(swap[:, :, half:DR], rr[:, :, 0:half].broadcast_to([P, TERMS, half]))
                ins.then_inc(weights_ready, 1)
                dve.wait_ge(weights_ready, L + 1)

            class Order:

                def __init__(self, steps, row):
                    self.steps, self.row, self.n = steps, row, 0

                def step(self, ins):
                    self.steps.by(ins)
                    self.n += 1
                    self.steps.wait(dve, self.row, self.n)

            def norm(step, src, dst):
                apart(dve)
                for t in range(NT):
                    ins = dve.bn_stats(stats[:, t, :], src(t))
                step(ins)
                apart(dve)
                for t in range(NT):
                    ins = dve.bn_aggr(mv[:, t, :], stats[:, t, :])
                step(ins)
                v, y, z = nwt[:, 0, :], nwt[:, 1, :], nwt[:, 2, :]
                step(dve.tensor_scalar(v, mv[:, :, 1], EPS, None, ALU.add))
                step(dve.tensor_scalar(y.bitcast(I32), v.bitcast(I32), -0.5, float(0x5F3759DF), ALU.mult, ALU.add))
                for _ in range(3):
                    step(dve.scalar_tensor_tensor(out=z, in0=y, scalar=-0.5, in1=y, op0=ALU.mult, op1=ALU.mult))
                    step(dve.tensor_tensor(z, z, v, ALU.mult))
                    step(dve.scalar_tensor_tensor(out=y, in0=z, scalar=1.5, in1=y, op0=ALU.add, op1=ALU.mult))
                for t in range(NT):
                    ins = dve.tensor_scalar(dst[:, t, :], src(t), mv[:, t, 0:1], nwt[:, 1, t:t + 1], ALU.subtract, ALU.mult)
                return ins

            def x_of(row):
                return lambda t: x[:, bass.ds(row.index(), 1), t, :].rearrange("p a d -> p (a d)")

            def x_row(row):
                return x[:, bass.ds(row.index(), 1), :, :].rearrange("p a t d -> p (a t d)")

            def low(src, dst, n, hi):
                k = dst.shape[0]
                return dve.scalar_tensor_tensor(out=r32(dst), in0=src, scalar=cst[0:k, C_SG + 2 * n + 1:C_SG + 2 * n + 2],
                                                in1=hi, op0=ALU.mult, op1=ALU.add)

            def prep(order, L, part):
                if order is None:
                    return
                row = order.row
                if part == "norm":
                    X[L].full[0].wait_before(dve, row)
                    xn_ready[L].by(norm(order.step, x_of(row), xn))
                elif part[0] == "rope":
                    _, w, v = part
                    X[0].wait(dve, row, part)
                    if (w, v) == (0, 0):
                        pv_done[0].wait_before(dve, row)
                    table = cst[0:ROPE, (C_COS, C_SIN)[v]:(C_COS, C_SIN)[v] + T]
                    X[0].take(part, dve.tensor_tensor(tmp[v], p_x[0:ROPE, :], table, ALU.mult))
                    if v == 1:
                        X[0].wait_taken(dve, row, part)
                        rot_ready[0].by(dve.tensor_tensor(tmp[0], tmp[0], tmp[1], ALU.add))
                        rot_ready[0].wait(dve, row, w + 1)
                        hi_ready[0].wait(dve, row, w + 1)
                        S1[0].wait_full_before(dve, row)
                        rope_done[0].by(low(tmp[0], (q_op, k_op)[w][0:ROPE, 0, :], (SG_QR, SG_KR)[w], tmp[2]))
                        rope_done[0].wait(dve, row, w + 1)
                elif part[0] == "heads":
                    _, g, w = part
                    X[L].wait(dve, row, part)
                    hi_ready[L].wait(dve, row, (2, 0)[L] + 2 * g + w + 1)
                    if L == 0:
                        if g >= 2:
                            dve.wait_ge(head_rows[g - 2], row.at(HEAD_ROWS, HEAD_ROWS))
                        elif row.before():
                            dve.wait_ge(head_rows[g + 2], row.at(HEAD_ROWS, 0))
                    elif w == 0:
                        S1[1].wait_full_before(dve, row)
                    else:
                        k_masked[1].wait_before(dve, row)
                    dst = stk[0:STACK, 2 * w + g % 2, :] if L == 0 else (q_op, stk)[w][0:STACK, g, :]
                    X[L].take(part, low(p_x[0:STACK, :], dst, ((SG_QN, SG_KN), (SG_Q1, SG_K1))[L][w], tmp[w]))

            def row_work(row, L, nxt):
                main = Order(main_step[L], row)
                after = None if nxt is None else Order(prep_step[L], nxt)
                step = main.step

                def prep_at(point):
                    for part in parts_at(L, point):
                        prep(after, L, part)

                def max_unit(n):
                    g, p, qt = n // 8, n // 4 % 2, n % 4
                    s = R[L].wait(dve, row, ("S", n))
                    hi = T if L else P * (qt + 1)
                    R[L].take(("S", n), dve.tensor_reduce(mneg[:, g % 2, qt, 2 * p:2 * p + 2], pairs[s][:, :, 0:hi],
                                                          axis=AX.X, op=ALU.max, negate=True))
                    if n % 8 == 7:
                        max_split(g)

                def max_split(g):
                    for n in (8 * g + 6, 8 * g + 7):
                        R[L].wait_taken(dve, row, ("S", n))
                    m = mneg[:, g % 2, :, :]
                    if L == 0:
                        hi, lo, m = mrow0[:, 0, :, :], mrow0[:, 1, :, :], m.rearrange("p q j -> p j q")
                    else:
                        hi, lo = mrow1[:, :, STACK:STACK + GH], mrow1[:, :, STACK + GH:K1]
                    step(dve.tensor_copy(r32(hi), m))
                    m_split[L].by(dve.tensor_tensor(r32(lo), m, hi, ALU.subtract))

                def max_rows(g):
                    M[L].wait(dve, row, ("mt", g))
                    if L == 0:
                        if g:
                            dve.wait_ge(m_rows[g - 1], row.at(M_ROWS, M_ROWS))
                        else:
                            dve.wait_ge(m_rows[NG - 1], row.at(M_ROWS, 1))
                        ins = dve.tensor_copy(r32(mT[:, :]), p_m[0:2 * GH * NT, 0:P])
                    else:
                        ins = dve.tensor_copy(r32(q_op[STACK:K1, g, :]), p_m[STACK:K1, :])
                    M[L].take(("mt", g), ins)

                def normalise(g):
                    M[L].wait(dve, row, ("ot", g))
                    o = p_m[:, :].rearrange("p (q j c) -> p q j c", q=NT, j=GH)
                    step(dve.reciprocal(rsum[:, :, :], o[:, :, :, HD]))
                    dst = onorm[:, :, :].rearrange("p q (g j d) -> p q g j d", g=NG, j=GH)[:, :, g, :, :]
                    M[L].take(("ot", g), dve.tensor_tensor(dst, o[:, :, :, 0:HD], rsum[:, :, :].unsqueeze(3).broadcast_to([P, NT, GH, HD]), ALU.mult))

                for n in range(AHEAD[L]):
                    max_unit(n)
                    if n == 9:
                        max_rows(0)
                for q in range(NQ):
                    if q in MT_AT[L]:
                        max_rows(MT_AT[L][q])
                    if q in OT_AT:
                        normalise(OT_AT[q])
                    for n in s_of(L, q):
                        max_unit(n)
                    if L == 0 and q == 12:
                        dve.wait_ge(loads[3], n_load[3])
                        dve.wait_ge(loads[2], n_load[2])
                    prep_at(("q", q))
                prep_at("out")
                normalise(NG - 1)
                prep_at("on")
                M[L].wait(dve, row, "proj")
                if L == 0:
                    ins = dve.tensor_scalar(hF[:, :], p_m[:, :], column(0, 2, row), None, ALU.mult)
                else:
                    ins = dve.tensor_scalar(hF[:, :], p_m[:, :], cols[:, R_BP:R_BP + 1], column(1, 2, row), ALU.add, ALU.mult)
                M[L].take("proj", ins)
                prep_at("proj")
                M[L].wait(dve, row, "xa")
                M[L].take("xa", dve.tensor_tensor(x_row(row), x_row(row), p_m[:, :], ALU.add))
                M[L].wait_taken(dve, row, "xa")
                on_ready[L].by(norm(step, x_of(row), onorm))

                E, k = EX[L], (TOP, 1)[L]
                left = 16 - E
                lgv, rm = lg[:, :, 0:E], rmax[:, 0, :]

                def wide(ap):
                    return ap.unsqueeze(2).broadcast_to([P, NT, E])

                if L == 0:
                    M[0].wait_taken(dve, row, "ln2")
                    h_lo_ready[0].by(dve.tensor_tensor(r32(h_lo[:, :]), hF[:, :], h_hi[:, :], ALU.subtract))
                M[L].wait(dve, row, "lg")
                M[L].take("lg", dve.tensor_tensor(lgv, p_m[:, 0:16 * NT].rearrange("p (t e) -> p t e", t=NT)[:, :, 0:E],
                                                  b_rt[L][:, :].unsqueeze(1).broadcast_to([P, NT, E]), ALU.add))
                M[L].wait_taken(dve, row, "lg")
                step(dve.tensor_reduce(rm, lgv, axis=AX.X, op=ALU.max))
                logits_ready[L].by(dve.tensor_tensor(lgv, lgv, wide(rm), ALU.subtract))
                if L == 1:
                    M[1].wait(dve, row, "hb")
                    M[1].take("hb", norm(step, lambda t: p_m[:, P * t:P * (t + 1)], onorm))
                prep_at("lg")
                rt_exp[L].wait(dve, row)
                step(dve.tensor_reduce(rmax[:, 1, :], pr[:, :, 0:E], axis=AX.X, op=ALU.add))
                step(dve.reciprocal(rm, rmax[:, 1, :]))
                step(dve.tensor_tensor(pw[:, :, left:16], pr[:, :, 0:E], wide(rm), ALU.mult))
                apart(dve)
                for t in range(NT):
                    ins = dve.max(top[:, t, :], pw[:, t, left:24])
                step(ins)
                step(dve.tensor_copy(topk[L][:, :, 0:k], top[:, :, 0:k]))
                apart(dve)
                for t in range(NT):
                    ins = dve.match_replace(pr[:, t, left:24], topk[L][:, t, :], pw[:, t, left:24], -2.0)
                step(ins)
                step(dve.scalar_tensor_tensor(out=gate[:, :, 0:E], in0=pr[:, :, left:16], scalar=-2.0, in1=pw[:, :, left:16],
                                              op0=ALU.is_equal, op1=ALU.mult))
                step(dve.tensor_copy(r32(gate2[:, :, 0:16]), gate[:, :, :]))
                gate_ready[L].by(dve.tensor_tensor(r32(gate2[:, :, 16:32]), gate[:, :, :], gate2[:, :, 0:16], ALU.subtract))
                if L == 1:
                    M[1].wait_taken(dve, row, "ln3")
                    h_lo_ready[1].by(dve.tensor_tensor(r32(h_lo[:, :]), hF[:, :], h_hi[:, :], ALU.subtract))
                else:
                    step(dve.tensor_scalar(hF[:, :], hF[:, :], column(0, 5, row), None, ALU.mult))
                prep_at("gt")
                M[L].wait(dve, row, "gt")
                M[L].take("gt", dve.tensor_copy(r32(gateT[0:32, :]), p_m[0:32, :]))

                def hidden_lo(i):
                    g_hi[L].wait(dve, row, i + 1)
                    kk = i % DEPTH
                    g_lo[L].by(dve.tensor_tensor(r32(hid_lo[:, i % SPLIT, :, :]), ring[:, 2 * kk:2 * kk + 2, :],
                                                 hid_hi[:, i % SPLIT, :, :], ALU.subtract))

                for i in range(CU[L]):
                    e = expert_of(L, i)
                    if e is not None:
                        R[L].wait_taken(dve, row, ("h", i))
                        spread[L].wait(dve, row, e + 1)
                        full = ring[:, 2 * (i % DEPTH):2 * (i % DEPTH) + 2, :]
                        gated[L].by(dve.tensor_tensor(full, full, gates[e % 2][:, :].unsqueeze(1).broadcast_to([P, 2, T]), ALU.mult))
                    if i:
                        hidden_lo(i - 1)
                    prep_at(("u", i))
                hidden_lo(CU[L] - 1)

                y_step[L].wait(dve, row)
                if L == 0:
                    ins = dve.scalar_tensor_tensor(out=hF[:, :], in0=p_o[:, :], scalar=column(0, 5, row), in1=hF[:, :], op0=ALU.mult, op1=ALU.add)
                else:
                    ins = dve.tensor_scalar(hF[:, :], p_o[:, :], column(1, 5, row), None, ALU.mult)
                y_taken[L].by(ins)
                M[L].wait(dve, row, "xy")
                M[L].take("xy", dve.tensor_tensor(x_row(row), x_row(row), p_m[:, :], ALU.add))
                M[L].wait_taken(dve, row, "xy")

            for L in range(2):
                layer_start(dve, L)
                head_weights(L)
                if L == 0:
                    dve.wait_ge(pool_ready, POOL_SETUP)
                first = Order(prep_step[L], Row(0))
                for i, part in enumerate(PARTS[L]):
                    prep(first, L, part)
                    for n in pieces_after(L, i):
                        k, chunks, hi, lo = piece(L, n)
                        dve.wait_ge(w_hi, first_piece(L) + n + 1)
                        dve.tensor_tensor(r32(lo), stage[:, k, 0:chunks, :], hi, ALU.subtract).then_inc(w_lo, 1)
                with dve.Fori(0, NB - 1) as b:
                    row_work(Row(b), L, Row(b, 1))
                row_work(LAST, L, None)

        for name, s in signals.items():
            assert s.made == 2 * s.per, [(n, t.made, t.per) for n, t in signals.items() if t.made != 2 * t.per]


_INS = ['L0_attn_x', 'L0_attn_W_kv_down', 'L0_attn_W_k_up', 'L0_attn_W_v_up', 'L0_attn_W_q', 'L0_attn_W_q_rope',
        'L0_attn_W_k_rope', 'L0_attn_W_o', 'L0_ffn_sW1', 'L0_ffn_sb1', 'L0_ffn_sW2', 'L0_ffn_sb2', 'L0_ffn_rW1',
        'L0_ffn_rb1', 'L0_ffn_rW2', 'L0_ffn_rb2', 'L0_ffn_gW', 'L0_ffn_gb', 'L0_c', 'L0_wmod', 'L1_attn_w_qkv',
        'L1_attn_w_proj', 'L1_attn_b_proj', 'L1_ffn_Wr', 'L1_ffn_br', 'L1_ffn_ln_g', 'L1_ffn_ln_b', 'L1_ffn_W1',
        'L1_ffn_b1', 'L1_ffn_W2', 'L1_ffn_b2', 'L1_c', 'L1_wmod']


def kernel(**inputs):
    import concourse.bacc as _bacc
    from concourse.bass_utils import run_bass_kernel_spmd as _run

    nc = _bacc.Bacc("TRN2", target_bir_lowering=False, num_devices=1)
    arrays, args = {}, {}
    for name in _INS:
        arrays[f"in_{name}_dram"] = v = np.ascontiguousarray(inputs[name])
        args[name] = nc.dram_tensor(f"in_{name}_dram", v.shape, mybir.dt.from_np(v.dtype), kind="ExternalInput").ap()
    arrays["const_dram"] = c = constants()
    args["const"] = nc.dram_tensor("const_dram", c.shape, F32, kind="ExternalInput").ap()
    out = nc.dram_tensor("out_dram", (NB, T, D), F32, kind="ExternalOutput").ap()
    build(nc, args, out)
    r = _run(nc, [arrays], core_ids=[0])
    return r.results[0]["out_dram"]
```

```python
from contextlib import ExitStack

import concourse.bass as bass
import numpy as np
from concourse import mybir

F32 = mybir.dt.float32
F32R = mybir.dt.float32r
BF16 = mybir.dt.bfloat16
I32 = mybir.dt.int32
ALU = mybir.AluOpType
ACT = mybir.ActivationFunctionType
AX = mybir.AxisListType

P = 128
NB, T, D = 4, 512, 128
NT = T // P
H, HD = 16, 8
DR = 32
NG, GH = 4, 4
E0, E1 = 15, 8
TOP = 3
C0, C1 = 2 * E0 + 4, 4 * E1
TERMS = 3
STACK = TERMS * GH * HD
ROPE = TERMS * DR
NOPE = TERMS * HD
K0 = ROPE + NOPE + 2
K1 = STACK + 2 * GH
SETS = 3
SCALE0 = 1.0 / float(np.sqrt(HD + DR))
SCALE1 = float(HD) ** -0.5
MASKED = -1e30
EPS = 1e-5

C_ID, C_MS, C_MT, C_HM, C_SG = 0, P, 2 * P, 3 * P, 3 * P + GH
C_SEL = C_SG + 12
C_COS = C_SEL + 16
C_SIN = C_COS + T
C_N = C_SIN + T
SG_Q1, SG_K1, SG_QN, SG_KN, SG_QR, SG_KR = range(6)
R_B0, R_B1, R_LNG, R_LNB, R_BP, R_C = 0, C0, C0 + C1, C0 + C1 + 1, C0 + C1 + 2, C0 + C1 + 3
R_N = R_C + 2 * NB
PREP_STEPS = [13, 13]
MAIN_STEPS = [30, 43]


def constants():
    c = np.zeros((P, C_N), np.float32)
    p = np.arange(P)
    c[:, C_ID:C_ID + P] = np.eye(P)
    c[:, C_MS:C_MS + P] = np.where(p[None, :] > p[:, None], MASKED, 0)
    c[:, C_MT:C_MT + P] = np.where(p[:, None] > p[None, :], MASKED, 0)
    c[:, C_SEL:C_SEL + 16] = (p[:, None] < 32) & (p[:, None] % 16 == np.arange(16)[None, :])
    for j in range(GH):
        own = ((p < STACK) & (p % (GH * HD) // HD == j)) | (p == STACK + j) | (p == STACK + GH + j)
        c[:, C_HM + j] = own

    def split(n, low, scale):
        c[:, C_SG + 2 * n] = np.where(low, -scale, scale)
        c[:, C_SG + 2 * n + 1] = np.where(low, scale, 0)

    split(SG_Q1, p // (GH * HD) == 2, SCALE1)
    split(SG_K1, p // (GH * HD) == 1, 1.0)
    split(SG_QN, p % NOPE // HD == 2, SCALE0)
    split(SG_KN, p % NOPE // HD == 1, 1.0)
    split(SG_QR, p // DR == 2, SCALE0)
    split(SG_KR, p // DR == 1, 1.0)
    inv = (np.float32(1.0) / np.float32(10000.0) ** (np.arange(0, DR, 2, dtype=np.float32) / np.float32(DR))).astype(np.float32)
    f = np.outer(np.arange(T, dtype=np.float32), inv).astype(np.float32).T
    c[:ROPE, C_COS:C_COS + T] = np.tile(np.cos(f), (2 * TERMS, 1))
    c[:ROPE, C_SIN:C_SIN + T] = np.tile(np.concatenate([-np.sin(f), np.sin(f)]), (TERMS, 1))
    return c


class Row:

    def __init__(self, b, off=0):
        self.b, self.off = b, off

    def index(self):
        return self.b + self.off

    def at(self, per, k):
        return self.b * per + (self.off * per + k)

    def before(self):
        return None if isinstance(self.b, int) and self.b + self.off == 0 else Row(self.b, self.off - 1)


class Signal:

    def __init__(self, sem, per):
        self.sem, self.per, self.made = sem, per, 0

    def _wait(self, eng, value):
        eng.wait_ge(self.sem, value)
        if eng.engine == mybir.EngineType.SP:
            eng.nop(nofuse=True)

    def by(self, ins):
        ins.then_inc(self.sem, 1)
        self.made += 1
        return ins

    def wait(self, eng, row, k=None):
        self._wait(eng, row.at(self.per, (self.per if k is None else k) + 1))

    def wait_before(self, eng, row):
        self._wait(eng, row.at(self.per, 1))


class Ring:

    def __init__(self, sig, name, order, slots):
        self.where, n = {}, [0] * slots
        for i, unit in enumerate(order):
            assert unit not in self.where, unit
            self.where[unit] = (i % slots, n[i % slots])
            n[i % slots] += 1
        self.full = [sig(f"{name}{s}_full", n[s]) for s in range(slots)]
        self.taken = [sig(f"{name}{s}_taken", n[s]) for s in range(slots)]

    def open(self, eng, row, unit):
        s, k = self.where[unit]
        self.taken[s].wait(eng, row, k)
        return s

    def fill(self, unit, ins):
        self.full[self.where[unit][0]].by(ins)

    def wait(self, eng, row, unit):
        s, k = self.where[unit]
        self.full[s].wait(eng, row, k + 1)
        return s

    def take(self, unit, ins):
        self.taken[self.where[unit][0]].by(ins)

    def wait_taken(self, eng, row, unit):
        s, k = self.where[unit]
        self.taken[s].wait(eng, row, k + 1)

    def wait_full_before(self, eng, row):
        for f in self.full:
            f.wait_before(eng, row)


NS = NG * (GH // 2) * NT
NQ = NG * NT
AHEAD = [14, 10]
S_PACE = [[2, 2, 2, 2, 2, 0, 2, 2, 2, 2, 0, 0, 0, 0, 0, 0],
          [2, 2, 2, 2, 2, 2, 2, 2, 2, 2, 2, 0, 0, 0, 0, 0]]
MT_AT = [{1: 1, 5: 2, 10: 3}, {3: 1, 7: 2, 11: 3}]
OT_AT = {6: 0, 9: 1, 13: 2}
CU = [C0 // 2, C1 // 2]
EX = [E0, E1]
UNITS = [1, 2]
DEPTH = 3
SPLIT = 2
STAGES, STAGE = 3, 8
PIECES = [[(which, lo, min(lo + STAGE, hi)) for which in range(2) for lo0, hi in ((0, 2 * E0), (2 * E0, C0))
           for lo in range(lo0, hi, STAGE)],
          [(which, lo, lo + STAGE) for which in range(2) for lo in range(0, C1, STAGE)]]

HEADS = [("heads", g, w) for g in range(NG) for w in range(2)]
ROPES = [("rope", w, v) for w in range(2) for v in range(2)]
PREP = [["norm", "ln1", "ckv"] + ROPES + HEADS + ["v"], ["norm", "ln1"] + HEADS + ["v"]]
NORM_TAIL = ["n1", "n2", "n3"]
NORM_2 = ["m1", "m2", "m3"]
TAIL = [{"ot": 0, "on": 1, "proj": 2, "xa": 4, "ns": 5, "n1": 6, "n2": 7, "n3": 8, "ln2": 10, "lg": 14, "ex": 18, "hin": 19},
        {"ot": 0, "on": 1, "proj": 2, "xa": 3, "ns": 4, "n1": 5, "n2": 6, "n3": 7, "ln2": 9, "lg": 10, "ex": 10, "hb": 11,
         "m1": 12, "m2": 13, "rt1": 13, "m3": 14, "rt2": 15, "ln3": 16, "gt": 17, "hin": 18}]
STEPS = [CU[L] + DEPTH for L in range(2)]
ROTATED = [("rope", 1, 0), ("heads", 0, 0)]
LATE = 13
LEAD = 6
XY_AT, RT_AT, GT_AT = 9, 7, 9
ROPE_K0 = 6


def tail_at(L, u):
    return [part for part, at in TAIL[L].items() if at == u]


def prep_at(L, u):
    return PREP[L][1 + u] if 1 + u < len(PREP[L]) else None


def s_of(L, q):
    first = AHEAD[L] + sum(S_PACE[L][:q])
    return list(range(first, first + S_PACE[L][q]))


def misc_order(L):
    out = [("mt", 0)]
    for q in range(NQ):
        if q in MT_AT[L]:
            out.append(("mt", MT_AT[L][q]))
        if q in OT_AT:
            out.append(("ot", OT_AT[q]))
    return out + [("ot", NG - 1), "on", "proj", "xa", "ln2", "lg"] + ([], ["hb", "ln3"])[L] + ["gt"]


def expert_of(L, i):
    return (i if i < E0 else None) if L == 0 else i // 2


def build(nc, a, out):
    ctx = ExitStack()
    with ctx:
        def sb(name, shape, dt=F32):
            return ctx.enter_context(nc.sbuf_tensor(name, shape, dt))

        def sem(name):
            return ctx.enter_context(nc.semaphore(name))

        signals = {}

        def sig(name, per):
            signals[name] = Signal(sem(name), per)
            return signals[name]

        def layers(name, per0, per1):
            return [sig(f"{name}_{L}", per) if per else None for L, per in enumerate((per0, per1))]

        cst = sb("cst", [P, C_N])
        cols = sb("cols", [P, R_N])
        w_kvd, w_vup, w_o = (sb(n, [P, P]) for n in ("w_kvd", "w_vup", "w_o"))
        w_rope = sb("w_rope", [P, 2, 2, ROPE])
        w_head = sb("w_head", [P, 2, NG, STACK])
        w_qkv = sb("w_qkv", [P, 3 * D])
        w_proj = sb("w_proj", [P, D])
        w12 = sb("w12", [P, 2, 2, C0, P])
        w_rt = [sb("w_rt0", [P, E0]), sb("w_rt1", [P, E1])]
        b_rt = [sb("b_rt0", [P, E0]), sb("b_rt1", [P, E1])]
        b_2 = sb("b_2", [P, 2, D])
        sel = sb("sel", [P, 16])
        id_r = sb("id_r", [P, P])
        id_bf = sb("id_bf", [P, P], BF16)
        mask_bf = sb("mask_bf", [P, 2, P], BF16)
        silu = sb("silu", [P, 3, 2 * NB])
        modT = sb("modT", [P, 2, 6, NB])
        guard = sb("guard", [P, 2, 2, NB])
        x = sb("x", [P, NB, NT, D])
        stats = sb("stats", [P, NT, 6])
        mv = sb("mv", [P, NT, 2])
        nwt = sb("nwt", [P, 3, NT])
        xn = sb("xn", [P, NT, D])
        hT = sb("hT", [P, T])
        ckvT = sb("ckvT", [P, T])
        q_op = sb("q_op", [P, SETS * GH, T])
        k_op = sb("k_op", [P, SETS * GH, T])
        stk = sb("stk", [P, 4, T])
        vaug = sb("vaug", [P, NT, H, HD + 1])
        ring = sb("ring", [P, 8, T])
        hid_hi = sb("hid_hi", [P, SPLIT, 2, T])
        hid_lo = sb("hid_lo", [P, SPLIT, 2, T])
        mneg = sb("mneg", [P, 2, NT, GH])
        mrow0 = sb("mrow0", [P, 2, GH, NT])
        mrow1 = sb("mrow1", [P, NT, K1])
        mT = sb("mT", [2 * GH * NT, P])
        oT = sb("oT", [P, T])
        rsum = sb("rsum", [P, NT, GH])
        onorm = sb("onorm", [P, NT, D])
        hF = sb("hF", [P, T])
        yT = sb("yT", [P, T])
        h_hi = sb("h_hi", [P, T])
        h_lo = sb("h_lo", [P, T])
        lg = sb("lg", [P, NT, 16])
        pw = sb("pw", [P, NT, 24])
        pr = sb("pr", [P, NT, 24])
        rmax = sb("rmax", [P, 2, NT])
        top = sb("top", [P, NT, 8])
        topk = [sb("topk0", [P, NT, 8]), sb("topk1", [P, NT, 8])]
        gate = sb("gate", [P, NT, 16])
        gate2 = sb("gate2", [P, NT, 32])
        gateT = sb("gateT", [P, T])
        tmp = [ring[0:ROPE, 6, :], ring[0:ROPE, 7, :], oT[0:ROPE, :]]
        rows = oT[0:R_N, 0:P]
        stage = ring[:, 0:6, :].rearrange("p s t -> p (s t)").rearrange("p (k c n) -> p k c n", k=STAGES, n=P)
        w_mod = x[:, 1:, :, :].rearrange("p b t d -> p (b t d)").rearrange("p (l j n) -> p l j n", l=2, j=6)
        raw = onorm[:, :, :].rearrange("p t d -> p (t d)")
        w_q, w_kup, w_rr = raw[:, 0:D], raw[:, D:2 * D], raw[:, 2 * D:2 * D + 2 * DR].rearrange("p (w r) -> p w r", w=2)

        pairs = [ctx.enter_context(nc.psum_tensor(f"pair{i}", [P, 2, T], F32)) for i in range(2)]
        singles = [ctx.enter_context(nc.psum_tensor(f"single{i}", [P, T], F32)) for i in range(2)]
        p_o = ctx.enter_context(nc.psum_tensor("p_o", [P, T], F32))
        p_m = ctx.enter_context(nc.psum_tensor("p_m", [P, T], F32))
        p_g = singles[1]
        p_x = singles[0]

        RS = [Ring(sig, f"max_{L}_", [("S", n) for n in range(NS)], 2) for L in range(2)]
        RH = [Ring(sig, f"hid_{L}_", [("h", i) for i in range(CU[L])], 2) for L in range(2)]
        S1 = [Ring(sig, f"single_{L}_", [("ST", n) for n in range(NQ * GH)], 2) for L in range(2)]
        M = [Ring(sig, f"misc_{L}_", misc_order(L), 1) for L in range(2)]
        X = [Ring(sig, f"prep_{L}_", PREP[L][1:], 1) for L in range(2)]
        Y = [Ring(sig, f"out_{L}_", ["xy"], 1) for L in range(2)]

        loads = [sem(f"load{i}") for i in range(4)]
        n_load = [0] * 4
        pool_ready = sem("pool_ready")
        cols_full, cols_ready, exp_c, silu_ready = (sem(n) for n in ("cols_full", "cols_ready", "exp_c", "silu_ready"))
        mod_full, mod_ready, weights_ready = (sem(n) for n in ("mod_full", "mod_ready", "weights_ready"))
        setup_step = sem("setup_step")
        staged = [sem(f"staged{k}") for k in range(STAGES)]
        w_hi, w_lo = sem("w_hi"), sem("w_lo")
        prep_step = layers("prep_step", *PREP_STEPS)
        main_step = layers("main_step", *MAIN_STEPS)
        xn_ready = layers("xn_ready", 1, 1)
        on_ready = layers("on_ready", 1, 1)
        rot_ready = layers("rot_ready", 2, 0)
        rope_done = layers("rope_done", 2, 0)
        rope_q = layers("rope_q", 1, 0)
        rope_k = layers("rope_k", SETS * GH - 1, 0)
        hi_ready = layers("hi_ready", 2 + 2 * NG, 2 * NG)
        head_rows = [sem(f"head_rows{g}") for g in range(NG)]
        HEAD_ROWS = 16 * 2 * GH
        k_masked = layers("k_masked", 0, GH * NG)
        m_split = layers("m_split", NG, NG)
        m_rows = [sem(f"m_rows{g}") for g in range(NG)]
        M_ROWS = 16 * 2
        pv_done = layers("pv_done", NQ, NQ)
        oT_ready = layers("oT_ready", NG, NG)
        logits_ready = layers("logits_ready", 1, 1)
        rt_exp = layers("rt_exp", 1, 1)
        gate_ready = layers("gate_ready", 1, 1)
        spread = layers("spread", *EX)
        h_hi_ready = layers("h_hi_ready", 1, 1)
        h_lo_ready = layers("h_lo_ready", 1, 1)
        gated = layers("gated", E0, C1 // 2)
        g_hi = layers("g_hi", *CU)
        g_lo = layers("g_lo", *CU)
        y_step = layers("y_step", *CU)
        y_taken = layers("y_taken", 1, 1)
        stored = sem("stored")

        block = ctx.enter_context(nc.Block())

        def r32(ap):
            return ap.bitcast(F32R)

        def apart(eng):
            eng.nop(nofuse=True)

        def slot(g, j=0):
            return g % SETS * GH + j

        def column(L, j, row):
            return modT[:, L, j, bass.ds(row.index(), 1)]

        def last_st(eng, row, L, n):
            S1[L].wait(eng, row, ("ST", n - 1))
            S1[L].wait(eng, row, ("ST", n))

        LAST = Row(NB - 1)

        def layer_start(eng, L):
            if L == 1:
                Y[0].wait_taken(eng, LAST, "xy")

        def first_piece(L):
            return L * len(PIECES[0])

        def piece(L, n):
            which, lo, hi = PIECES[L][n]
            return (first_piece(L) + n) % STAGES, hi - lo, w12[:, which, 0, lo:hi, :], w12[:, which, 1, lo:hi, :]

        def work(eng, attention, phase, close):
            attention(Row(0), None, None)
            phase(None, Row(0), Row(1))
            attention(Row(1), Row(0), None)
            with eng.Fori(0, NB - 2) as b:
                phase(Row(b), Row(b, 1), Row(b, 2))
                attention(Row(b, 2), Row(b, 1), Row(b))
            phase(LAST.before(), LAST, None)
            close(LAST, LAST.before())
            phase(LAST, None, None)
            close(None, LAST)

        def lead_at(L, u):
            n = 2 * (u - CU[L])
            return range(n, min(n + 2, LEAD)) if n >= 0 else ()

        def pieces_after(L, i):
            n = i - (4, 1)[L]
            last = i == len(PREP[L]) - 1
            return range(max(n, 0), len(PIECES[L])) if last else [n] if 0 <= n < len(PIECES[L]) else []

        @block.sync
        def _(sp):
            def load(i, dst, src):
                sp.dma_start(dst, src).then_inc(loads[i], 16)
                n_load[i] += 16

            load(0, cst[:, :], a["const"])
            small = [(R_B0, a["L0_ffn_rb1"].rearrange("e (c p) -> (e c) p", p=P)),
                     (R_B0 + 2 * E0, a["L0_ffn_sb1"].rearrange("e (c p) -> (e c) p", p=P)),
                     (R_B1, a["L1_ffn_b1"].rearrange("e (c p) -> (e c) p", p=P)),
                     (R_LNG, a["L1_ffn_ln_g"].rearrange("(a d) -> a d", a=1)),
                     (R_LNB, a["L1_ffn_ln_b"].rearrange("(a d) -> a d", a=1)),
                     (R_BP, a["L1_attn_b_proj"].rearrange("(a d) -> a d", a=1)),
                     (R_C, a["L0_c"]), (R_C + NB, a["L1_c"])]
            for r, src in small:
                load(0, rows[r:r + src.shape[0], :], src)
            for L in range(2):
                load(0, w_mod[:, L, :, :], a[f"L{L}_wmod"].rearrange("d (j n) -> d j n", j=6))
            load(0, x[:, 0, :, :], a["L0_attn_x"][0].rearrange("(t p) d -> p t d", p=P))
            for dst, name in ((w_kvd[:, :], "W_kv_down"), (w_q, "W_q"), (w_kup, "W_k_up"), (w_vup[:, :], "W_v_up"),
                              (w_o[:, :], "W_o"), (w_rr[:, 0, :], "W_q_rope"), (w_rr[:, 1, :], "W_k_rope")):
                load(1, dst, a[f"L0_attn_{name}"])

            def expert_loads(L):
                for n, (which, lo, hi) in enumerate(PIECES[L]):
                    if first_piece(L) + n >= STAGES:
                        sp.wait_ge(w_lo, first_piece(L) + n + 1 - STAGES)
                    k, per = (first_piece(L) + n) % STAGES, (2, 4)[L]
                    dst = stage[:, k, 0:hi - lo, :]
                    if lo == 2 * E0 and L == 0:
                        src = a["L0_ffn_sW1"][0] if which == 0 else a["L0_ffn_sW2"][0].rearrange("(c p) d -> p c d", p=P)
                        dst = dst.rearrange("p c n -> p (c n)") if which == 0 else dst
                    elif which == 0:
                        src = a[("L0_ffn_rW1", "L1_ffn_W1")[L]][lo // per:hi // per].rearrange("e d f -> d e f")
                        dst = dst.rearrange("p (e c) n -> p e (c n)", c=per)
                    else:
                        src = a[("L0_ffn_rW2", "L1_ffn_W2")[L]][lo // per:hi // per].rearrange("e (c p) d -> p (e c) d", p=P)
                    sp.dma_start(dst, src).then_inc(staged[k], 16)

            expert_loads(0)
            def m_dma(row, g):
                M[0].wait_taken(sp, row, ("mt", g))
                for part in range(2):
                    sp.dma_start(q_op[K0 - 2 + part:K0 - 1 + part, slot(g):slot(g) + GH, :],
                                 mT[GH * NT * part:GH * NT * (part + 1), :]).then_inc(m_rows[g], 16)

            def head_dma(row, g):
                if g >= SETS:
                    last_st(sp, row, 0, 16 * (g - SETS) + 15)
                else:
                    S1[0].wait_full_before(sp, row)
                for w, dst in enumerate((q_op, k_op)):
                    X[0].wait_taken(sp, row, ("heads", g, w))
                    for j in range(GH):
                        sp.dma_start(dst[ROPE:ROPE + NOPE, slot(g, j), :],
                                     stk[NOPE * j:NOPE * (j + 1), 2 * w + g % 2, :]).then_inc(head_rows[g], 16)

            def main(row):
                m_dma(row, 0)
                m_dma(row, 1)
                head_dma(row, SETS)
                m_dma(row, 2)
                m_dma(row, 3)

            for g in range(SETS):
                head_dma(Row(0), g)
            sp.wait_ge(pool_ready, 3)
            for r in (0, 16):
                load(2, b_2[r:r + E0, 0, :], a["L0_ffn_rb2"])
                load(2, b_2[r + E0:r + E0 + 1, 0, :], a["L0_ffn_sb2"])
                load(2, b_2[r:r + E1, 1, :], a["L1_ffn_b2"])
            for L, (rw, rb) in enumerate((("L0_ffn_gW", "L0_ffn_gb"), ("L1_ffn_Wr", "L1_ffn_br"))):
                load(2, w_rt[L][:, :], a[rw])
                load(2, b_rt[L][:, :], a[rb].partition_broadcast(P))
            N_G, GI, GO = a["L1_attn_w_qkv"].shape
            for g in range(N_G):
                load(2, w_qkv[GI * g:GI * (g + 1), GO * g:GO * (g + 1)], a["L1_attn_w_qkv"][g])
                load(2, w_proj[GI * g:GI * (g + 1), GI * g:GI * (g + 1)], a["L1_attn_w_proj"][g])
            sp.wait_ge(mod_full, 1)
            for b in range(1, NB):
                load(3, x[:, b, :, :], a["L0_attn_x"][b].rearrange("(t p) d -> p t d", p=P))
            with sp.Fori(0, NB - 1) as b:
                main(Row(b))
                for g in range(SETS):
                    head_dma(Row(b, 1), g)
            main(LAST)
            layer_start(sp, 1)
            expert_loads(1)
            with sp.Fori(0, NB) as b:
                Y[1].wait_taken(sp, Row(b), "xy")
                sp.dma_start(out[bass.ds(b, 1), :, :].rearrange("a (t p) d -> p (a t) d", p=P),
                             x[:, bass.ds(b, 1), :, :].rearrange("p a t d -> p (a t) d")).then_inc(stored, 16)
            sp.wait_ge(stored, 16 * NB)

        constant = [(w_qkv[:, :], 0.0), (w_proj[:, :], 0.0), (b_2[:, :, :], 0.0),
                    (vaug[:, :, :, HD:HD + 1], 1.0), (mrow1[:, :, :], 0.0), (stk[ROPE:P, :, :], 1.0), (k_op[ROPE:P, :, :], 1.0),
                    (gate[:, :, :], 1.0), (pw[:, :, :], -1.0), (topk[0][:, :, :], -1.0), (topk[1][:, :, :], -1.0), (gateT[:, :], 0.0)]
        POOL_SETUP = len(constant)

        @block.gpsimd
        def _(pool):
            for n, (dst, value) in enumerate(constant):
                pool.memset(dst, value).then_inc(pool_ready, 1)
                pool.wait_ge(pool_ready, n + 1)
            for s in signals.values():
                pool.sem_inc(s.sem, 1)
            pool.sem_inc(m_rows[NG - 1], 1)
            pool.wait_ge(loads[0], n_load[0])

            def spread_rope(row):
                rope_done[0].wait(pool, row, 1)
                S1[0].wait_full_before(pool, row)
                apart(pool)
                rope_q[0].by(pool.tensor_copy(r32(q_op[0:ROPE, 1:, :]), q_op[0:ROPE, 0:1, :].broadcast_to([ROPE, SETS * GH - 1, T])))

            def mask(row, g):
                X[1].wait_taken(pool, row, ("heads", g, 1))
                if g >= SETS:
                    last_st(pool, row, 1, 16 * (g - SETS) + 15)
                else:
                    S1[1].wait_full_before(pool, row)
                apart(pool)
                for j in range(GH):
                    k_masked[1].by(pool.tensor_scalar(r32(k_op[0:K1, slot(g, j), :]), stk[0:K1, g, :],
                                                      cst[0:K1, C_HM + j:C_HM + j + 1], None, ALU.mult))

            spread_rope(Row(0))
            with pool.Fori(0, NB - 1) as b:
                spread_rope(Row(b, 1))
            layer_start(pool, 1)
            for g in range(SETS):
                mask(Row(0), g)
            with pool.Fori(0, NB - 1) as b:
                mask(Row(b), SETS)
                for g in range(SETS):
                    mask(Row(b, 1), g)
            mask(LAST, SETS)

        @block.scalar
        def _(act):
            act.wait_ge(cols_ready, 1)
            act.activation(silu[:, 1, :], cols[:, R_C:R_C + 2 * NB], ACT.Exp, scale=-1.0).then_inc(exp_c, 1)
            act.wait_ge(mod_ready, 1)
            act.wait_ge(loads[0], n_load[0])

            def high(L, dst, src, n):
                hi_ready[L].by(act.activation(r32(dst), src, ACT.Copy,
                                              scale=cst[0:dst.shape[0], C_SG + 2 * n:C_SG + 2 * n + 1]))

            def prep(row, L, part):
                if part in (None, "norm"):
                    return
                if L == 0 and part in ROTATED:
                    w = ROTATED.index(part)
                    rot_ready[0].wait(act, row, w + 1)
                    if w == 1:
                        rope_done[0].wait(act, row, 1)
                    elif row.before():
                        M[0].wait(act, row.before(), "proj")
                    high(0, tmp[2], tmp[0], (SG_QR, SG_KR)[w])
                if part == "ln1":
                    X[L].wait(act, row, part)
                    X[L].full[0].wait_before(act, row)
                    X[L].take(part, act.activation(hT[:, :], p_x[:, :], ACT.Identity, bias=column(L, 0, row), scale=column(L, 1, row)))
                elif part == "ckv":
                    X[L].wait(act, row, part)
                    X[L].take(part, act.activation(ckvT[:, :], p_x[:, :], ACT.Copy))
                elif part == "v":
                    X[L].wait(act, row, part)
                    pv_done[L].wait_before(act, row)
                    X[L].take(part, act.activation(vaug[:, :, :, 0:HD], p_x[:, :].rearrange("p (t h d) -> p t h d", t=NT, d=HD), ACT.Copy))
                elif part[0] == "heads":
                    _, g, w = part
                    X[L].wait(act, row, part)
                    if g:
                        X[L].wait_taken(act, row, ("heads", g - 1, w))
                    elif L == 0:
                        rope_done[0].wait(act, row)
                    else:
                        pv_done[1].wait_before(act, row)
                    high(L, tmp[w], p_x[0:STACK, :], ((SG_QN, SG_KN), (SG_Q1, SG_K1))[L][w])

            def spread_rope(row, n):
                rope_done[0].wait(act, row)
                S1[0].wait_full_before(act, row)
                rope_k[0].by(act.activation(r32(k_op[0:ROPE, n, :]), k_op[0:ROPE, 0, :], ACT.Copy))

            def out_rows(row, L, g):
                pv_done[L].wait(act, row, NT * (g + 1))
                if g:
                    M[L].wait(act, row, ("ot", g - 1))
                else:
                    M[L].full[0].wait_before(act, row)
                oT_ready[L].by(act.activation(oT[:, :], p_o[:, :], ACT.Copy))

            def close(tail_row, moe, L):
                if moe:
                    y_step[L].wait(act, moe)
                    Y[L].full[0].wait_before(act, moe)
                    y_taken[L].by(act.activation(yT[:, :], p_o[:, :], ACT.Copy, scale=column(L, 5, moe)))
                if tail_row and L == 0:
                    tail(tail_row, L, "gt")

            def attention(row, tail_row, moe, L):
                close(tail_row, moe, L)
                M[L].wait(act, row, ("mt", 0))
                if L == 0:
                    act.wait_ge(m_rows[NG - 1], row.at(M_ROWS, 1))
                    ins = act.activation(r32(mT[:, :]), p_m[0:2 * GH * NT, 0:P], ACT.Copy)
                else:
                    ins = act.activation(r32(q_op[STACK:K1, 0, :]), p_m[STACK:K1, :], ACT.Copy)
                M[L].take(("mt", 0), ins)
                if row.before():
                    g_lo[L].wait_before(act, row.before())
                X[L].taken[0].wait(act, row)
                quads(row, L, range(LATE))

            def quads(row, L, which):
                for q in which:
                    g, kc = q // NT, q % NT
                    lo = P * kc if L == 0 else 0
                    for j in range(GH):
                        n = GH * q + j
                        s = S1[L].wait(act, row, ("ST", n))
                        if j == 0 and q >= 2:
                            pv_done[L].wait(act, row, q - 1)
                        S1[L].take(("ST", n), act.activation(ring[:, n % 8, lo:T], singles[s][:, lo:T], ACT.Exp))
                    if q >= NT and kc == 0:
                        out_rows(row, L, g - 1)

            def tail(row, L, part):
                if part == "on":
                    M[L].wait(act, row, "on")
                    M[L].take("on", act.activation(oT[:, :], p_m[:, :], ACT.Copy))
                elif part in ("ln2", "ln3"):
                    M[L].wait(act, row, part)
                    shift, scale = (column(L, 3, row), column(L, 4, row)) if part == "ln2" else \
                        (cols[:, R_LNB:R_LNB + 1], cols[:, R_LNG:R_LNG + 1])
                    M[L].take(part, act.activation(hF[:, :], p_m[:, :], ACT.Identity, bias=shift, scale=scale))
                elif part == "ex":
                    logits_ready[L].wait(act, row)
                    rt_exp[L].by(act.activation(pr[:, :, 0:EX[L]], lg[:, :, 0:EX[L]], ACT.Exp))
                elif part == "gt":
                    M[L].wait(act, row, "gt")
                    spread[L].wait_before(act, row)
                    M[L].take("gt", act.activation(r32(gateT[0:32, :]), p_m[0:32, :], ACT.Copy))
                elif part == "hin":
                    RH[L].wait_full_before(act, row)
                    M[L].wait_taken(act, row, ("ln2", "ln3")[L])
                    h_hi_ready[L].by(act.activation(r32(h_hi[:, :]), hF[:, :], ACT.Copy))

            def phase(moe, row, nxt, L):

                def hidden_hi(i):
                    if expert_of(L, i) is None:
                        RH[L].wait_taken(act, moe, ("h", i))
                    else:
                        gated[L].wait(act, moe, i + 1)
                    if i == 0:
                        y_step[L].wait_before(act, moe)
                    elif i >= SPLIT:
                        y_step[L].wait(act, moe, i - SPLIT + 1)
                    k = i % DEPTH
                    g_hi[L].by(act.activation(r32(hid_hi[:, i % SPLIT, :, :]), ring[:, 2 * k:2 * k + 2, :], ACT.Copy))

                if row:
                    quads(row, L, range(LATE, NQ))
                    out_rows(row, L, NG - 1)
                for u in range(STEPS[L]):
                    if moe and u < CU[L]:
                        s = RH[L].wait(act, moe, ("h", u))
                        if u >= DEPTH:
                            g_lo[L].wait(act, moe, u - DEPTH + 1)
                        for c in range(2):
                            col = (R_B0, R_B1)[L] + 2 * u + c
                            ins = act.activation(ring[:, 2 * (u % DEPTH) + c, :], pairs[s][:, c, :],
                                                 (ACT.Gelu, ACT.Relu)[L], bias=cols[:, col:col + 1])
                        RH[L].take(("h", u), ins)
                    if moe and 1 <= u <= CU[L]:
                        hidden_hi(u - 1)
                    if row:
                        for part in tail_at(L, u):
                            tail(row, L, part)
                    if nxt:
                        prep(nxt, L, prep_at(L, u))
                        if L == 0 and 0 <= u - ROPE_K0 < SETS * GH - 1:
                            spread_rope(nxt, 1 + u - ROPE_K0)

            for L in range(2):
                layer_start(act, L)
                for i, part in enumerate(PREP[L]):
                    prep(Row(0), L, part)
                    for n in pieces_after(L, i):
                        k, chunks, hi, _ = piece(L, n)
                        act.wait_ge(staged[k], 16 * ((first_piece(L) + n) // STAGES + 1))
                        act.activation(r32(hi), stage[:, k, 0:chunks, :], ACT.Copy).then_inc(w_hi, 1)
                    if L == 0 and part[0] == "heads":
                        for n in range(1 + (i - 7) * 3 // 2, min(SETS * GH, 1 + (i - 6) * 3 // 2)):
                            spread_rope(Row(0), n)
                work(act, lambda *rows_of: attention(*rows_of, L), lambda *rows_of: phase(*rows_of, L), lambda *left: close(*left, L))

        @block.tensor
        def _(pe):
            ident = cst[:, C_ID:C_ID + P]
            pe.wait_ge(loads[0], n_load[0])
            pe.transpose(p_m[:, 0:R_N], rows[:, :], cst[0:R_N, C_ID:C_ID + R_N]).then_inc(cols_full, 1)
            pe.wait_ge(silu_ready, 1)
            for L in range(2):
                for j in range(6):
                    n = (6 * L + j) * NB
                    ins = pe.matmul(p_o[:, n:n + NB], w_mod[:, L, j, :], silu[:, 0, NB * L:NB * (L + 1)], start=True, stop=True)
            ins.then_inc(mod_full, 1)
            pe.wait_ge(mod_ready, 1)

            def turn(dst, src):
                for t in range(NT):
                    ins = pe.transpose(dst[:, P * t:P * (t + 1)], src[:, t, :], ident)
                return ins

            def tiles(ap):
                return ap.rearrange("p (t n) -> p t n", t=NT)

            def prep(row, L, part):
                if part in (None, "norm"):
                    return
                if part == "ln1":
                    xn_ready[L].wait(pe, row)
                    S1[L].taken[0].wait_before(pe, row)
                X[L].open(pe, row, part)
                if part == "ln1":
                    ins = turn(p_x, xn)
                elif part == "ckv":
                    ins = pe.matmul(p_x[:, :], w_kvd[:, :], hT[:, :], start=True, stop=True)
                elif part == "v":
                    for t in range(NT):
                        src = (ckvT, hT)[L][:, P * t:P * (t + 1)]
                        ins = pe.matmul(p_x[:, P * t:P * (t + 1)], src, w_qkv[:, 2 * D:3 * D] if L else w_vup[:, :],
                                        start=True, stop=True)
                elif part[0] == "rope":
                    _, w, v = part
                    ins = pe.matmul(p_x[0:ROPE, :], w_rope[:, w, v, :], (hT, ckvT)[w][:, :], start=True, stop=True)
                else:
                    _, g, w = part
                    ins = pe.matmul(p_x[0:STACK, :], w_head[:, w, g, :], (ckvT if L == 0 and w else hT)[:, :], start=True, stop=True)
                X[L].fill(part, ins)

            def operands(row, L, g):
                if L == 0:
                    if g == 0:
                        rope_q[0].wait(pe, row)
                        rope_k[0].wait(pe, row)
                    pe.wait_ge(head_rows[g], row.at(HEAD_ROWS, HEAD_ROWS))
                else:
                    k_masked[1].wait(pe, row, GH * (g + 1))

            def scores(dst, L, lhs, rhs, lhs_lo, lo, hi, diagonal, kind):
                K = (K0, K1)[L]
                if kind == "S":
                    K = (K0 - 2, STACK)[L]
                ins = pe.matmul(dst[:, lo:hi], r32(lhs[0:K, lhs_lo:lhs_lo + P]), r32(rhs[0:K, lo:hi]), start=True, stop=L == 1)
                if L == 0:
                    ins = pe.matmul(dst[:, diagonal:diagonal + P], id_bf[:, :], mask_bf[:, 0 if kind == "S" else 1, :],
                                    start=False, stop=True)
                return ins

            def max_unit(row, L, n):
                g, p, qt = n // 8, n // 4 % 2, n % 4
                if n % 8 == 0:
                    operands(row, L, g)
                if n < 2 and row.before():
                    RH[L].taken[n].wait_before(pe, row.before())
                s = RS[L].open(pe, row, ("S", n))
                hi = T if L else max(2 * P, P * (qt + 1))
                for i in range(2):
                    j = 2 * p + i
                    qs = q_op[:, g, :] if L else q_op[:, slot(g, j), :]
                    ins = scores(pairs[s][:, i, :], L, qs, k_op[:, slot(g, j), :], P * qt, 0, hi, P * qt, "S")
                RS[L].fill(("S", n), ins)

            def max_turn(row, L, g):
                m_split[L].wait(pe, row, g + 1)
                M[L].open(pe, row, ("mt", g))
                if L == 0:
                    ins = pe.transpose(p_m[0:2 * GH * NT, 0:P], mrow0[:, :, :, :].rearrange("p a j q -> p (a j q)"), ident)
                else:
                    for t in range(NT):
                        ins = pe.transpose(p_m[0:K1, P * t:P * (t + 1)], mrow1[:, t, :], ident)
                M[L].fill(("mt", g), ins)

            def exp_unit(row, L, n):
                g, kc, j = n // 16, n // 4 % 4, n % 4
                if n % 16 == 0:
                    if L == 0:
                        pe.wait_ge(m_rows[g], row.at(M_ROWS, M_ROWS + (g == NG - 1)))
                    else:
                        M[1].wait_taken(pe, row, ("mt", g))
                if n == 0:
                    X[L].taken[0].wait(pe, row)
                elif n == 1 and row.before():
                    Y[L].taken[0].wait_before(pe, row.before())
                s = S1[L].open(pe, row, ("ST", n))
                qs = q_op[:, g, :] if L else q_op[:, slot(g, j), :]
                lo = 0 if L else min(2 * P, P * kc)
                S1[L].fill(("ST", n), scores(singles[s], L, k_op[:, slot(g, j), :], qs, P * kc, lo, T, P * kc, "ST"))

            def values(row, L, q):
                g, kc = q // NT, q % NT
                S1[L].wait_taken(pe, row, ("ST", GH * q + GH - 2))
                S1[L].wait_taken(pe, row, ("ST", GH * q + GH - 1))
                if q == 0:
                    if row.before():
                        y_taken[L].wait_before(pe, row.before())
                elif kc == 0:
                    oT_ready[L].wait(pe, row, g)
                lo = 0 if L else P * kc
                for j in range(GH):
                    ins = pe.matmul(p_o[32 * j:32 * j + HD + 1, lo:T], vaug[:, kc, GH * g + j, :], ring[:, (GH * q + j) % 8, lo:T],
                                    start=(kc == 0), stop=(kc == NT - 1))
                pv_done[L].by(ins)

            def out_turn(row, L, g):
                oT_ready[L].wait(pe, row, g + 1)
                M[L].open(pe, row, ("ot", g))
                M[L].fill(("ot", g), turn(p_m, tiles(oT[:, :])))

            def close(tail_row, moe, L, n):
                if n == XY_AT and moe:
                    y_taken[L].wait(pe, moe)
                    gated[L].wait(pe, moe)
                    Y[L].open(pe, moe, "xy")
                    Y[L].fill("xy", turn(p_g, tiles(yT[:, :])))
                if n == GT_AT and tail_row and L == 0:
                    tail(tail_row, L, "gt")

            def attention(row, tail_row, moe, L):
                for n in range(LEAD if tail_row else 0, AHEAD[L]):
                    close(tail_row, moe, L, n)
                    max_unit(row, L, n)
                    if n == 9:
                        max_turn(row, L, 0)
                quads(row, L, range(LATE))

            def quads(row, L, which):
                for q in which:
                    s_units = s_of(L, q)
                    for j in range(GH):
                        exp_unit(row, L, GH * q + j)
                        if j == 1:
                            if q:
                                values(row, L, q - 1)
                            if q in MT_AT[L]:
                                max_turn(row, L, MT_AT[L][q])
                            if q in OT_AT:
                                out_turn(row, L, OT_AT[q])
                        if s_units and (j != 1 if L == 0 else j == 3):
                            for n in s_units[0:1 + L]:
                                max_unit(row, L, s_units.pop(0))

            def tail(row, L, part):
                if part == "ot":
                    out_turn(row, L, NG - 1)
                    return
                if part not in M[L].where:
                    return
                if part == "ln2":
                    on_ready[L].wait(pe, row)
                elif part == "gt":
                    gate_ready[L].wait(pe, row)
                M[L].open(pe, row, part)
                if part in ("on", "ln2", "ln3"):
                    ins = turn(p_m, onorm)
                elif part == "proj":
                    ins = pe.matmul(p_m[:, :], (w_o, w_proj)[L][:, :], oT[:, :], start=True, stop=True)
                elif part in ("xa", "hb"):
                    ins = turn(p_m, tiles(hF[:, :]))
                elif part == "lg":
                    if L == 0:
                        pe.wait_ge(loads[2], n_load[2])
                    for t in range(NT):
                        ins = pe.matmul(p_m[:, 16 * t:16 * t + EX[L]], hF[:, P * t:P * (t + 1)], w_rt[L][:, :], start=True, stop=True)
                else:
                    for t in range(NT):
                        ins = pe.transpose(p_m[0:32, P * t:P * (t + 1)], gate2[:, t, :], ident)
                M[L].fill(part, ins)

            def phase(moe, row, nxt, L):
                def hidden(i):
                    if i < 2:
                        RS[L].taken[i].wait(pe, row or LAST)
                    s = RH[L].open(pe, moe, ("h", i))
                    for c in range(2):
                        n = 2 * i + c
                        hi, lo = (r32(w12[:, 0, part, n, :]) for part in range(2))
                        pe.matmul(pairs[s][:, c, :], hi, r32(h_hi[:, :]), start=True, stop=False)
                        pe.matmul(pairs[s][:, c, :], hi, r32(h_lo[:, :]), start=False, stop=False)
                        ins = pe.matmul(pairs[s][:, c, :], lo, r32(h_hi[:, :]), start=False, stop=True)
                    RH[L].fill(("h", i), ins)

                def spread_gate(e):
                    if e == 0:
                        S1[L].wait_taken(pe, row or LAST, ("ST", NQ * GH - 1))
                        Y[L].taken[0].wait_before(pe, moe)
                    else:
                        gated[L].wait(pe, moe, UNITS[L] * e)
                    spread[L].by(pe.matmul(p_g[:, :], r32(sel[:, e:e + 1].broadcast_to([P, P])), r32(gateT[:, :]), start=True, stop=True))

                def second(i):
                    g_lo[L].wait(pe, moe, i + 1)
                    k = i % SPLIT
                    for c in range(2):
                        n = 2 * i + c
                        hi, lo = (r32(w12[:, 1, part, n, :]) for part in range(2))
                        rest = hid_lo[:, k, c, :]
                        pe.matmul(p_o[:, :], hi, r32(hid_hi[:, k, c, :]), start=False, stop=False)
                        pe.matmul(p_o[:, :], hi, r32(rest), start=False, stop=False)
                        ins = pe.matmul(p_o[:, :], lo, r32(hid_hi[:, k, c, :]), start=False, stop=(n == 2 * CU[L] - 1))
                    y_step[L].by(ins)

                if moe:
                    pe.wait_ge(w_lo, first_piece(L) + len(PIECES[L]))
                    h_lo_ready[L].wait(pe, moe)
                if row:
                    for q in range(LATE, NQ):
                        quads(row, L, [q])
                        if moe and q - LATE in (0, 1):
                            hidden(q - LATE)
                    values(row, L, NQ - 1)
                if moe:
                    M[L].wait_taken(pe, moe, "gt")
                for u in range(STEPS[L]):
                    if moe:
                        if u < CU[L] and (u >= 2 or not row):
                            hidden(u)
                        if u >= DEPTH:
                            second(u - DEPTH)
                        if u < CU[L] and expert_of(L, u) is not None and u % UNITS[L] == 0:
                            spread_gate(expert_of(L, u))
                        if u == 0:
                            oT_ready[L].wait(pe, row or LAST)
                            y_taken[L].wait_before(pe, moe)
                            pe.matmul(p_o[:, :], b_2[:, L, :], gateT[:, :], start=True, stop=False)
                            if L == 0:
                                pe.matmul(p_o[:, :], r32(id_r[:, :]), r32(h_hi[:, :]), start=False, stop=False)
                                pe.matmul(p_o[:, :], r32(id_r[:, :]), r32(h_lo[:, :]), start=False, stop=False)
                    if row:
                        for part in tail_at(L, u):
                            tail(row, L, part)
                    if nxt:
                        prep(nxt, L, prep_at(L, u))
                        for n in lead_at(L, u):
                            max_unit(nxt, L, n)

            for L in range(2):
                layer_start(pe, L)
                pe.wait_ge(weights_ready, L + 1)
                for part in PREP[L]:
                    prep(Row(0), L, part)
                work(pe, lambda *rows_of: attention(*rows_of, L), lambda *rows_of: phase(*rows_of, L),
                     lambda *left: [close(*left, L, n) for n in range(AHEAD[L] + 1)])

        @block.vector
        def _(dve):
            n_setup = [0]

            def settle(ins):
                ins.then_inc(setup_step, 1)
                n_setup[0] += 1
                dve.wait_ge(setup_step, n_setup[0])

            dve.wait_ge(cols_full, 1)
            dve.tensor_copy(cols[:, :], p_m[:, 0:R_N]).then_inc(cols_ready, 1)
            dve.wait_ge(exp_c, 1)
            settle(dve.tensor_scalar(silu[:, 2, :], silu[:, 1, :], 1.0, None, ALU.add))
            settle(dve.reciprocal(silu[:, 1, :], silu[:, 2, :]))
            dve.wait_ge(cols_ready, 1)
            dve.tensor_tensor(silu[:, 0, :], silu[:, 1, :], cols[:, R_C:R_C + 2 * NB], ALU.mult).then_inc(silu_ready, 1)
            dve.tensor_copy(id_bf[:, :], cst[:, C_ID:C_ID + P])
            dve.tensor_copy(r32(sel[:, :]), cst[:, C_SEL:C_SEL + 16])
            dve.tensor_copy(r32(id_r[:, :]), cst[:, C_ID:C_ID + P])
            dve.tensor_copy(mask_bf[:, :, :], cst[:, C_MS:C_MS + 2 * P].rearrange("p (a n) -> p a n", a=2))
            dve.wait_ge(mod_full, 1)
            settle(dve.tensor_copy(modT[:, :, :, :].rearrange("p l j b -> p (l j b)"), p_o[:, 0:12 * NB]))
            dve.memset(p_o[:, :], 0.0)
            gg = modT[:, :, 2:6:3, :]
            settle(dve.tensor_scalar(guard[:, :, :, :], gg, 0.0, 2.0, ALU.is_ge, ALU.mult))
            settle(dve.scalar_tensor_tensor(out=gg, in0=gg, scalar=-1.0, in1=gg, op0=ALU.mult, op1=ALU.max))
            settle(dve.tensor_scalar(gg, gg, 0.25, None, ALU.max))
            settle(dve.scalar_tensor_tensor(out=gg, in0=guard[:, :, :, :], scalar=-1.0, in1=gg, op0=ALU.add, op1=ALU.mult))
            dve.tensor_scalar(modT[:, :, 1, :], modT[:, :, 1, :], 1.0, None, ALU.add)
            dve.tensor_scalar(modT[:, :, 4, :], modT[:, :, 4, :], 1.0, None, ALU.add).then_inc(mod_ready, 1)
            dve.wait_ge(mod_ready, 1)
            dve.wait_ge(loads[0], n_load[0])

            def head_weights(L):
                dve.wait_ge(loads[1], n_load[1])
                for w in range(2):
                    for t in range(TERMS):
                        if L == 0:
                            src = (w_q, w_kup)[w].rearrange("p (g h d) -> p g h d", g=NG, d=HD)
                            dst = w_head[:, w, :, :].rearrange("p g (h c) -> p g h c", c=NOPE)[:, :, :, HD * t:HD * (t + 1)]
                            for g in range(NG):
                                ins = dve.tensor_copy(dst[:, g, :, :], src[:, g, :, :])
                        else:
                            ins = dve.tensor_copy(w_head[:, w, :, GH * HD * t:GH * HD * (t + 1)],
                                                  w_qkv[:, D * w:D * (w + 1)].rearrange("p (g n) -> p g n", g=NG))
                    if L == 0:
                        plain = w_rope[:, w, 0, :].rearrange("p (t r) -> p t r", t=TERMS)
                        swap = w_rope[:, w, 1, :].rearrange("p (t r) -> p t r", t=TERMS)
                        rr, half = w_rr[:, w, :].unsqueeze(1), DR // 2
                        dve.tensor_copy(plain, rr.broadcast_to([P, TERMS, DR]))
                        dve.tensor_copy(swap[:, :, 0:half], rr[:, :, half:DR].broadcast_to([P, TERMS, half]))
                        ins = dve.tensor_copy(swap[:, :, half:DR], rr[:, :, 0:half].broadcast_to([P, TERMS, half]))
                ins.then_inc(weights_ready, 1)
                dve.wait_ge(weights_ready, L + 1)

            class Order:

                def __init__(self, steps, row, n=0):
                    self.steps, self.row, self.n = steps, row, n

                def step(self, ins):
                    self.steps.by(ins)
                    self.n += 1
                    self.steps.wait(dve, self.row, self.n)

            def norm_start(step, src):
                apart(dve)
                for t in range(NT):
                    ins = dve.bn_stats(stats[:, t, :], src(t))
                step(ins)
                apart(dve)
                for t in range(NT):
                    ins = dve.bn_aggr(mv[:, t, :], stats[:, t, :])
                step(ins)
                v, y = nwt[:, 0, :], nwt[:, 1, :]
                step(dve.tensor_scalar(v, mv[:, :, 1], EPS, None, ALU.add))
                step(dve.tensor_scalar(y.bitcast(I32), v.bitcast(I32), -0.5, float(0x5F3759DF), ALU.mult, ALU.add))

            def newton(step):
                v, y, z = nwt[:, 0, :], nwt[:, 1, :], nwt[:, 2, :]
                step(dve.scalar_tensor_tensor(out=z, in0=y, scalar=-0.5, in1=y, op0=ALU.mult, op1=ALU.mult))
                step(dve.tensor_tensor(z, z, v, ALU.mult))
                step(dve.scalar_tensor_tensor(out=y, in0=z, scalar=1.5, in1=y, op0=ALU.add, op1=ALU.mult))

            def norm_end(src, dst):
                for t in range(NT):
                    ins = dve.tensor_scalar(dst[:, t, :], src(t), mv[:, t, 0:1], nwt[:, 1, t:t + 1], ALU.subtract, ALU.mult)
                return ins

            def x_of(row):
                return lambda t: x[:, bass.ds(row.index(), 1), t, :].rearrange("p a d -> p (a d)")

            def x_row(row):
                return x[:, bass.ds(row.index(), 1), :, :].rearrange("p a t d -> p (a t d)")

            def low(src, dst, n, hi):
                k = dst.shape[0]
                return dve.scalar_tensor_tensor(out=r32(dst), in0=src, scalar=cst[0:k, C_SG + 2 * n + 1:C_SG + 2 * n + 2],
                                                in1=hi, op0=ALU.mult, op1=ALU.add)

            def prep(order, L, part):
                if part is None:
                    return
                row = order.row
                if part == "norm":
                    X[L].full[0].wait_before(dve, row)
                    norm_start(order.step, x_of(row))
                    for _ in range(3):
                        newton(order.step)
                    xn_ready[L].by(norm_end(x_of(row), xn))
                if L == 0 and part in ROTATED:
                    w = ROTATED.index(part)
                    rot_ready[0].wait(dve, row, w + 1)
                    hi_ready[0].wait(dve, row, w + 1)
                    S1[0].wait_full_before(dve, row)
                    rope_done[0].by(low(tmp[0], (q_op, k_op)[w][0:ROPE, 0, :], (SG_QR, SG_KR)[w], tmp[2]))
                    rope_done[0].wait(dve, row, w + 1)
                if part[0] == "rope":
                    _, w, v = part
                    X[0].wait(dve, row, part)
                    if (w, v) == (0, 0):
                        pv_done[0].wait_before(dve, row)
                    table = cst[0:ROPE, (C_COS, C_SIN)[v]:(C_COS, C_SIN)[v] + T]
                    X[0].take(part, dve.tensor_tensor(tmp[v], p_x[0:ROPE, :], table, ALU.mult))
                    if v == 1:
                        X[0].wait_taken(dve, row, part)
                        rot_ready[0].by(dve.tensor_tensor(tmp[0], tmp[0], tmp[1], ALU.add))
                elif part[0] == "heads":
                    _, g, w = part
                    X[L].wait(dve, row, part)
                    hi_ready[L].wait(dve, row, (2, 0)[L] + 2 * g + w + 1)
                    if L == 0:
                        if g >= 2:
                            dve.wait_ge(head_rows[g - 2], row.at(HEAD_ROWS, HEAD_ROWS))
                        elif row.before():
                            dve.wait_ge(head_rows[g + 2], row.at(HEAD_ROWS, 0))
                    elif w == 0:
                        S1[1].wait_full_before(dve, row)
                    else:
                        k_masked[1].wait_before(dve, row)
                    dst = stk[0:STACK, 2 * w + g % 2, :] if L == 0 else (q_op, stk)[w][0:STACK, g, :]
                    X[L].take(part, low(p_x[0:STACK, :], dst, ((SG_QN, SG_KN), (SG_Q1, SG_K1))[L][w], tmp[w]))

            def max_unit(row, L, n):
                g, p, qt = n // 8, n // 4 % 2, n % 4
                s = RS[L].wait(dve, row, ("S", n))
                hi = T if L else P * (qt + 1)
                RS[L].take(("S", n), dve.tensor_reduce(mneg[:, g % 2, qt, 2 * p:2 * p + 2], pairs[s][:, :, 0:hi],
                                                       axis=AX.X, op=ALU.max, negate=True))

            def close(tail_order, moe, L, n):
                if n == XY_AT and moe:
                    Y[L].wait(dve, moe, "xy")
                    Y[L].take("xy", dve.tensor_tensor(x_row(moe), x_row(moe), p_g[:, :], ALU.add))
                if L == 0 and tail_order and n == RT_AT:
                    tail(tail_order, L, "rt1")
                    tail(tail_order, L, "rt2")

            def attention(main, left, moe, L):
                for n in range(LEAD if left else 0, AHEAD[L]):
                    close(left, moe, L, n)
                    max_unit(main.row, L, n)
                    if n % 8 == 7:
                        max_split(main, L, n // 8)
                quads(main, L, range(LATE))

            def quads(main, L, which):
                for q in which:
                    if q in MT_AT[L]:
                        max_rows(main.row, L, MT_AT[L][q])
                    if q in OT_AT:
                        normalise(main.row, L, OT_AT[q], main.step)
                    for n in s_of(L, q):
                        max_unit(main.row, L, n)
                        if n % 8 == 7:
                            max_split(main, L, n // 8)

            def max_split(main, L, g):
                row, step = main.row, main.step
                for n in (8 * g + 6, 8 * g + 7):
                    RS[L].wait_taken(dve, row, ("S", n))
                m = mneg[:, g % 2, :, :]
                if L == 0:
                    hi, lo, m = mrow0[:, 0, :, :], mrow0[:, 1, :, :], m.rearrange("p q j -> p j q")
                else:
                    hi, lo = mrow1[:, :, STACK:STACK + GH], mrow1[:, :, STACK + GH:K1]
                step(dve.tensor_copy(r32(hi), m))
                m_split[L].by(dve.tensor_tensor(r32(lo), m, hi, ALU.subtract))

            def max_rows(row, L, g):
                M[L].wait(dve, row, ("mt", g))
                if L == 0:
                    dve.wait_ge(m_rows[g - 1], row.at(M_ROWS, M_ROWS))
                    ins = dve.tensor_copy(r32(mT[:, :]), p_m[0:2 * GH * NT, 0:P])
                else:
                    ins = dve.tensor_copy(r32(q_op[STACK:K1, g, :]), p_m[STACK:K1, :])
                M[L].take(("mt", g), ins)

            def normalise(row, L, g, step):
                M[L].wait(dve, row, ("ot", g))
                o = p_m[:, :].rearrange("p (q j c) -> p q j c", q=NT, j=GH)
                step(dve.reciprocal(rsum[:, :, :], o[:, :, :, HD]))
                dst = onorm[:, :, :].rearrange("p q (g j d) -> p q g j d", g=NG, j=GH)[:, :, g, :, :]
                M[L].take(("ot", g), dve.tensor_tensor(dst, o[:, :, :, 0:HD], rsum[:, :, :].unsqueeze(3).broadcast_to([P, NT, GH, HD]), ALU.mult))

            def tail(main, L, part):
                row, step = main.row, main.step
                E, k = EX[L], (TOP, 1)[L]
                left = 16 - E
                lgv, rm = lg[:, :, 0:E], rmax[:, 0, :]

                def wide(ap):
                    return ap.unsqueeze(2).broadcast_to([P, NT, E])

                if part == "ot":
                    normalise(row, L, NG - 1, step)
                elif part == "proj":
                    M[L].wait(dve, row, "proj")
                    if L == 0:
                        ins = dve.tensor_scalar(hF[:, :], p_m[:, :], column(0, 2, row), None, ALU.mult)
                    else:
                        ins = dve.tensor_scalar(hF[:, :], p_m[:, :], cols[:, R_BP:R_BP + 1], column(1, 2, row), ALU.add, ALU.mult)
                    M[L].take("proj", ins)
                elif part == "xa":
                    M[L].wait(dve, row, "xa")
                    M[L].take("xa", dve.tensor_tensor(x_row(row), x_row(row), p_m[:, :], ALU.add))
                elif part == "ns":
                    M[L].wait_taken(dve, row, "xa")
                    norm_start(step, x_of(row))
                elif part in NORM_TAIL + NORM_2:
                    newton(step)
                    if part == "n3":
                        on_ready[L].by(norm_end(x_of(row), onorm))
                    elif part == "m3":
                        M[1].take("hb", norm_end(lambda t: p_m[:, P * t:P * (t + 1)], onorm))
                elif part == "lg":
                    M[L].wait(dve, row, "lg")
                    M[L].take("lg", dve.tensor_tensor(lgv, p_m[:, 0:16 * NT].rearrange("p (t e) -> p t e", t=NT)[:, :, 0:E],
                                                      b_rt[L][:, :].unsqueeze(1).broadcast_to([P, NT, E]), ALU.add))
                    M[L].wait_taken(dve, row, "lg")
                    step(dve.tensor_reduce(rm, lgv, axis=AX.X, op=ALU.max))
                    logits_ready[L].by(dve.tensor_tensor(lgv, lgv, wide(rm), ALU.subtract))
                elif part == "hb":
                    M[1].wait(dve, row, "hb")
                    norm_start(step, lambda t: p_m[:, P * t:P * (t + 1)])
                elif part == "rt1":
                    rt_exp[L].wait(dve, row)
                    step(dve.tensor_reduce(rmax[:, 1, :], pr[:, :, 0:E], axis=AX.X, op=ALU.add))
                    step(dve.reciprocal(rm, rmax[:, 1, :]))
                    step(dve.tensor_tensor(pw[:, :, left:16], pr[:, :, 0:E], wide(rm), ALU.mult))
                    apart(dve)
                    for t in range(NT):
                        ins = dve.max(top[:, t, :], pw[:, t, left:24])
                    step(ins)
                elif part == "rt2":
                    step(dve.tensor_copy(topk[L][:, :, 0:k], top[:, :, 0:k]))
                    apart(dve)
                    for t in range(NT):
                        ins = dve.match_replace(pr[:, t, left:24], topk[L][:, t, :], pw[:, t, left:24], -2.0)
                    step(ins)
                    step(dve.scalar_tensor_tensor(out=gate[:, :, 0:E], in0=pr[:, :, left:16], scalar=-2.0, in1=pw[:, :, left:16],
                                                  op0=ALU.is_equal, op1=ALU.mult))
                    step(dve.tensor_copy(r32(gate2[:, :, 0:16]), gate[:, :, :]))
                    gate_ready[L].by(dve.tensor_tensor(r32(gate2[:, :, 16:32]), gate[:, :, :], gate2[:, :, 0:16], ALU.subtract))
                elif part == "hin":
                    h_hi_ready[L].wait(dve, row)
                    h_lo_ready[L].by(dve.tensor_tensor(r32(h_lo[:, :]), hF[:, :], h_hi[:, :], ALU.subtract))

            def phase(moe, main, nxt, L):
                def hidden_lo(i):
                    g_hi[L].wait(dve, moe, i + 1)
                    k = i % DEPTH
                    g_lo[L].by(dve.tensor_tensor(r32(hid_lo[:, i % SPLIT, :, :]), ring[:, 2 * k:2 * k + 2, :],
                                                 hid_hi[:, i % SPLIT, :, :], ALU.subtract))

                if main:
                    quads(main, L, range(LATE, NQ))
                if L == 0:
                    dve.wait_ge(loads[3], n_load[3])
                    dve.wait_ge(loads[2], n_load[2])
                if nxt:
                    prep(Order(prep_step[L], nxt), L, "norm")
                for u in range(STEPS[L]):
                    e = expert_of(L, u) if u < CU[L] else None
                    if moe and e is not None:
                        RH[L].wait_taken(dve, moe, ("h", u))
                        spread[L].wait(dve, moe, e + 1)
                        full = ring[:, 2 * (u % DEPTH):2 * (u % DEPTH) + 2, :]
                        gated[L].by(dve.tensor_tensor(full, full, p_g[:, :].unsqueeze(1).broadcast_to([P, 2, T]), ALU.mult))
                    if moe and 1 <= u <= CU[L]:
                        hidden_lo(u - 1)
                    if main:
                        for part in tail_at(L, u):
                            tail(main, L, part)
                    if nxt:
                        prep(Order(prep_step[L], nxt), L, prep_at(L, u))
                        for n in lead_at(L, u):
                            max_unit(nxt, L, n)

            for L in range(2):
                layer_start(dve, L)
                head_weights(L)
                if L == 0:
                    dve.wait_ge(pool_ready, POOL_SETUP)
                first = Order(prep_step[L], Row(0))
                for i, part in enumerate(PREP[L]):
                    prep(first, L, part)
                    for n in pieces_after(L, i):
                        k, chunks, hi, lo = piece(L, n)
                        dve.wait_ge(w_hi, first_piece(L) + n + 1)
                        dve.tensor_tensor(r32(lo), stage[:, k, 0:chunks, :], hi, ALU.subtract).then_inc(w_lo, 1)
                steps = {}

                def attend(row, tail_row, moe):
                    main = Order(main_step[L], row)
                    attention(main, tail_row and Order(main_step[L], tail_row, steps.get("tail")), moe, L)
                    steps["attention"] = main.n

                def run_phase(moe, row, nxt):
                    main = row and Order(main_step[L], row, steps["attention"])
                    phase(moe, main, nxt, L)
                    if row:
                        steps["tail"] = main.n

                def finish(tail_row, moe):
                    left = tail_row and Order(main_step[L], tail_row, steps["tail"])
                    for n in range(AHEAD[L] + 1):
                        close(left, moe, L, n)

                work(dve, attend, run_phase, finish)

        for name, s in signals.items():
            assert s.made in (2 * s.per, 3 * s.per), [(n, t.made, t.per) for n, t in signals.items() if t.made % t.per]


_INS = ['L0_attn_x', 'L0_attn_W_kv_down', 'L0_attn_W_k_up', 'L0_attn_W_v_up', 'L0_attn_W_q', 'L0_attn_W_q_rope',
        'L0_attn_W_k_rope', 'L0_attn_W_o', 'L0_ffn_sW1', 'L0_ffn_sb1', 'L0_ffn_sW2', 'L0_ffn_sb2', 'L0_ffn_rW1',
        'L0_ffn_rb1', 'L0_ffn_rW2', 'L0_ffn_rb2', 'L0_ffn_gW', 'L0_ffn_gb', 'L0_c', 'L0_wmod', 'L1_attn_w_qkv',
        'L1_attn_w_proj', 'L1_attn_b_proj', 'L1_ffn_Wr', 'L1_ffn_br', 'L1_ffn_ln_g', 'L1_ffn_ln_b', 'L1_ffn_W1',
        'L1_ffn_b1', 'L1_ffn_W2', 'L1_ffn_b2', 'L1_c', 'L1_wmod']


def kernel(**inputs):
    import concourse.bacc as _bacc
    from concourse.bass_utils import run_bass_kernel_spmd as _run

    nc = _bacc.Bacc("TRN2", target_bir_lowering=False, num_devices=1)
    arrays, args = {}, {}
    for name in _INS:
        arrays[f"in_{name}_dram"] = v = np.ascontiguousarray(inputs[name])
        args[name] = nc.dram_tensor(f"in_{name}_dram", v.shape, mybir.dt.from_np(v.dtype), kind="ExternalInput").ap()
    arrays["const_dram"] = c = constants()
    args["const"] = nc.dram_tensor("const_dram", c.shape, F32, kind="ExternalInput").ap()
    out = nc.dram_tensor("out_dram", (NB, T, D), F32, kind="ExternalOutput").ap()
    build(nc, args, out)
    r = _run(nc, [arrays], core_ids=[0])
    return r.results[0]["out_dram"]
```
